# Optimizing a Trainium2 kernel written in Bass

```python
import numpy as np
import jax
import jax.numpy as jnp

def _softmax(x, axis=-1):
    return jax.nn.softmax(x, axis=axis)
def _gelu(x):
    return jax.nn.gelu(x, approximate=True)
def _silu(x):
    return jax.nn.silu(x)
def _sigmoid(x):
    return jax.nn.sigmoid(x)
def _layernorm(x, axis=-1, eps=1e-5):
    m = jnp.mean(x, axis=axis, keepdims=True)
    v = jnp.var(x, axis=axis, keepdims=True)
    return (x - m) / jnp.sqrt(v + eps)
def _scatter_add(tgt, idx, src, axis=0):
    return tgt.at[idx].add(src)
def _segment_sum(src, seg, n):
    return jax.ops.segment_sum(src, seg, n)

kernel_name = 'mk_conv_attn_hybrid_d2_conv_nchw128_622d8a'

def setup_inputs(seed: int = 0):
    np.random.seed(seed)
    _w = jnp.asarray
    def _rec_inputs():
        import jax
        import jax.numpy as jnp
        _gk = jax.random.key(seed)
        x = -0.0005153 + 1.001 * jax.random.normal(jax.random.fold_in(_gk, 1), (32, 128, 28, 28), jnp.float32)
        return x
    x = _rec_inputs()
    def _L0_conv_setup():
        import jax, jax.numpy as jnp
        import numpy as np
        from jax import lax
        K = 3
        PAD = 1
        EPS = 1e-05
        THRESHOLD = 0.005

        def shift_quant(w, threshold=THRESHOLD):
            aw = jnp.abs(w)
            q = jnp.sign(w) * jnp.exp2(jnp.round(jnp.log2(jnp.maximum(aw, 1e-10))))
            q = jnp.where(aw < threshold, 0.0, q)
            return w + lax.stop_gradient(q - w)

        def shift_conv(x, w, stride=1):
            wq = shift_quant(w)
            return lax.conv_general_dilated(x, wq, window_strides=(stride, stride), padding=[(PAD, PAD), (PAD, PAD)], dimension_numbers=('NCHW', 'OIHW', 'NCHW'))

        def adder_conv(x, w):
            N, Cin, H, W = x.shape
            Cout = w.shape[0]
            patches = lax.conv_general_dilated_patches(x, filter_shape=(K, K), window_strides=(1, 1), padding=[(PAD, PAD), (PAD, PAD)])
            Ck = patches.shape[1]
            p = patches.reshape(N, Ck, H * W)
            wf = w.reshape(Cout, Ck)

            def per_channel(wc):
                return -jnp.sum(jnp.abs(p - wc[None, :, None]), axis=1)
            out = lax.map(per_channel, wf)
            return out.transpose(1, 0, 2).reshape(N, Cout, H, W)

        def batchnorm(x, gamma, beta):
            mean = jnp.mean(x, axis=(0, 2, 3), keepdims=True)
            var = jnp.var(x, axis=(0, 2, 3), keepdims=True)
            xn = (x - mean) * lax.rsqrt(var + EPS)
            return xn * gamma[None, :, None, None] + beta[None, :, None, None]
        key = jax.random.key(seed)
        ks = jax.random.split(key, 5)
        N, C, H, W = (32, 128, 28, 28)
        std = 1.0 / np.sqrt(C * K * K)
        x = jax.random.normal(ks[0], (N, C, H, W), dtype=jnp.float32)
        w_shift1 = jax.random.normal(ks[1], (C, C, K, K), dtype=jnp.float32) * std
        w_add1 = jax.random.normal(ks[2], (C, C, K, K), dtype=jnp.float32) * std
        w_shift2 = jax.random.normal(ks[3], (C, C, K, K), dtype=jnp.float32) * std
        w_add2 = jax.random.normal(ks[4], (C, C, K, K), dtype=jnp.float32) * std
        return {'x': x, 'w_shift1': w_shift1, 'w_add1': w_add1, 'bn1_gamma': jnp.ones((C,), jnp.float32), 'bn1_beta': jnp.zeros((C,), jnp.float32), 'w_shift2': w_shift2, 'w_add2': w_add2, 'bn2_gamma': jnp.ones((C,), jnp.float32), 'bn2_beta': jnp.zeros((C,), jnp.float32)}
    _L0_conv_all = _L0_conv_setup()
    _L0_conv_in = {k: v for k, v in _L0_conv_all.items() if k in ('w_shift1', 'w_add1', 'bn1_gamma', 'bn1_beta', 'w_shift2', 'w_add2', 'bn2_gamma', 'bn2_beta', )}
    del _L0_conv_all

    def _L1_attn_setup():
        import jax, jax.numpy as jnp
        import numpy as np
        B, T, D = (4, 2048, 128)
        key = jax.random.key(seed)
        k1, k2, k3 = jax.random.split(key, 3)
        x = jax.random.normal(k1, (B, T, D), dtype=jnp.float32)
        lim = 1.0 / np.sqrt(D)
        W = jax.random.uniform(k2, (3 * D, D), dtype=jnp.float32, minval=-lim, maxval=lim)
        b = jax.random.uniform(k3, (3 * D,), dtype=jnp.float32, minval=-lim, maxval=lim)
        return {'x': x, 'W': W, 'b': b}
    _L1_attn_all = _L1_attn_setup()
    _L1_attn_in = {k: v for k, v in _L1_attn_all.items() if k in ('W', 'b', )}
    del _L1_attn_all

    def _L1_ffn_setup():
        import jax, jax.numpy as jnp
        import numpy as np
        B, N, D, C, E, K = (8, 8192, 128, 128, 8, 2)
        key = jax.random.key(seed)
        k0, k1, k2 = jax.random.split(key, 3)
        x = jax.random.normal(k0, (B, N, D), dtype=jnp.float32)
        router_w = jax.random.normal(k1, (D, E), dtype=jnp.float32) * 0.05
        router_b = jnp.zeros((E,), dtype=jnp.float32)
        expert_w = jax.random.normal(k2, (E, D, C), dtype=jnp.float32) * (1.0 / np.sqrt(D))
        expert_b = jnp.zeros((E, C), dtype=jnp.float32)
        return {'x': x, 'router_w': router_w, 'router_b': router_b, 'expert_w': expert_w, 'expert_b': expert_b}
    _L1_ffn_all = _L1_ffn_setup()
    _L1_ffn_in = {k: v for k, v in _L1_ffn_all.items() if k in ('router_w', 'router_b', 'expert_w', 'expert_b', )}
    del _L1_ffn_all

    return {
        "x": x,
        "L0_conv_w_shift1": _L0_conv_in["w_shift1"],
        "L0_conv_w_add1": _L0_conv_in["w_add1"],
        "L0_conv_bn1_gamma": _L0_conv_in["bn1_gamma"],
        "L0_conv_bn1_beta": _L0_conv_in["bn1_beta"],
        "L0_conv_w_shift2": _L0_conv_in["w_shift2"],
        "L0_conv_w_add2": _L0_conv_in["w_add2"],
        "L0_conv_bn2_gamma": _L0_conv_in["bn2_gamma"],
        "L0_conv_bn2_beta": _L0_conv_in["bn2_beta"],
        "L1_attn_W": _L1_attn_in["W"],
        "L1_attn_b": _L1_attn_in["b"],
        "L1_ffn_router_w": _L1_ffn_in["router_w"],
        "L1_ffn_router_b": _L1_ffn_in["router_b"],
        "L1_ffn_expert_w": _L1_ffn_in["expert_w"],
        "L1_ffn_expert_b": _L1_ffn_in["expert_b"],
    }

def reference(x, L0_conv_w_shift1, L0_conv_w_add1, L0_conv_bn1_gamma, L0_conv_bn1_beta, L0_conv_w_shift2, L0_conv_w_add2, L0_conv_bn2_gamma, L0_conv_bn2_beta, L1_attn_W, L1_attn_b, L1_ffn_router_w, L1_ffn_router_b, L1_ffn_expert_w, L1_ffn_expert_b):
    import jax
    import jax.numpy as jnp
    def _L0_conv_ref(x, w_shift1, w_add1, bn1_gamma, bn1_beta, w_shift2, w_add2, bn2_gamma, bn2_beta):
        import jax, jax.numpy as jnp
        import numpy as np
        from jax import lax
        K = 3
        PAD = 1
        EPS = 1e-05
        THRESHOLD = 0.005

        def shift_quant(w, threshold=THRESHOLD):
            aw = jnp.abs(w)
            q = jnp.sign(w) * jnp.exp2(jnp.round(jnp.log2(jnp.maximum(aw, 1e-10))))
            q = jnp.where(aw < threshold, 0.0, q)
            return w + lax.stop_gradient(q - w)

        def shift_conv(x, w, stride=1):
            wq = shift_quant(w)
            return lax.conv_general_dilated(x, wq, window_strides=(stride, stride), padding=[(PAD, PAD), (PAD, PAD)], dimension_numbers=('NCHW', 'OIHW', 'NCHW'))

        def adder_conv(x, w):
            N, Cin, H, W = x.shape
            Cout = w.shape[0]
            patches = lax.conv_general_dilated_patches(x, filter_shape=(K, K), window_strides=(1, 1), padding=[(PAD, PAD), (PAD, PAD)])
            Ck = patches.shape[1]
            p = patches.reshape(N, Ck, H * W)
            wf = w.reshape(Cout, Ck)

            def per_channel(wc):
                return -jnp.sum(jnp.abs(p - wc[None, :, None]), axis=1)
            out = lax.map(per_channel, wf)
            return out.transpose(1, 0, 2).reshape(N, Cout, H, W)

        def batchnorm(x, gamma, beta):
            mean = jnp.mean(x, axis=(0, 2, 3), keepdims=True)
            var = jnp.var(x, axis=(0, 2, 3), keepdims=True)
            xn = (x - mean) * lax.rsqrt(var + EPS)
            return xn * gamma[None, :, None, None] + beta[None, :, None, None]
        residual = x
        out = adder_conv(shift_conv(x, w_shift1, stride=1), w_add1)
        out = jax.nn.relu(batchnorm(out, bn1_gamma, bn1_beta))
        out = adder_conv(shift_conv(out, w_shift2, stride=1), w_add2)
        out = batchnorm(out, bn2_gamma, bn2_beta)
        return jax.nn.relu(out + residual)

    def _L1_attn_ref(x, W, b):
        import jax, jax.numpy as jnp
        import numpy as np
        B, T, D = (4, 2048, 128)
        Bx, Tx, Dx = x.shape
        qkv = (x @ W.T + b).reshape(Bx, Tx, 3, Dx)
        q, k, v = (qkv[:, :, 0], qkv[:, :, 1], qkv[:, :, 2])
        q = jax.nn.elu(q) + 1.0
        k = jax.nn.elu(k) + 1.0
        kv = jnp.einsum('bti,btj->btij', k, v)
        kv_cum = jnp.cumsum(kv, axis=1)
        k_cum = jnp.cumsum(k, axis=1)
        num = jnp.einsum('bti,btij->btj', q, kv_cum)
        den = jnp.einsum('bti,bti->bt', q, k_cum)[..., None] + 1e-06
        return num / den

    def _L1_ffn_ref(x, router_w, router_b, expert_w, expert_b):
        import jax, jax.numpy as jnp
        import numpy as np
        B, N, D, C, E, K = (8, 8192, 128, 128, 8, 2)
        router_probs = jax.nn.softmax(x @ router_w + router_b, axis=-1)
        top_p, top_i = jax.lax.top_k(router_probs, K)
        top_p = top_p / jnp.sum(top_p, axis=-1, keepdims=True)
        expert_out = jnp.einsum('bnd,edc->bnec', x, expert_w) + expert_b
        gathered = jnp.take_along_axis(expert_out, top_i[..., None], axis=2)
        return jnp.einsum('bnk,bnkc->bnc', top_p, gathered)

    def _gn(v, G=32, eps=1e-5):
        B_, C_, H_, W_ = v.shape
        g = v.reshape(B_, G, C_ // G, H_, W_)
        m = jnp.mean(g, axis=(2, 3, 4), keepdims=True)
        s = jnp.var(g, axis=(2, 3, 4), keepdims=True)
        return ((g - m) / jnp.sqrt(s + eps)).reshape(v.shape)

    def _ln_c(v, eps=1e-6):
        m = jnp.mean(v, axis=1, keepdims=True)
        s = jnp.var(v, axis=1, keepdims=True)
        return (v - m) / jnp.sqrt(s + eps)

    def _ln_t(v, eps=1e-5):
        m = jnp.mean(v, axis=-1, keepdims=True)
        s = jnp.var(v, axis=-1, keepdims=True)
        return (v - m) / jnp.sqrt(s + eps)

    def _to_tokens(v):
        B_, C_, H_, W_ = v.shape
        return v.reshape(B_, C_, H_ * W_).transpose(0, 2, 1)
    def _from_tokens(t, like):
        B_, C_, H_, W_ = like.shape
        return t.transpose(0, 2, 1).reshape(B_, C_, H_, W_)

    x = _L0_conv_ref(x, L0_conv_w_shift1, L0_conv_w_add1, L0_conv_bn1_gamma, L0_conv_bn1_beta, L0_conv_w_shift2, L0_conv_w_add2, L0_conv_bn2_gamma, L0_conv_bn2_beta)
    t = _to_tokens(x)
    t = t + _L1_attn_ref(_ln_t(t), L1_attn_W, L1_attn_b)
    t = t + _L1_ffn_ref(_ln_t(t), L1_ffn_router_w, L1_ffn_router_b, L1_ffn_expert_w, L1_ffn_expert_b)
    x = _from_tokens(t, x)
    return x


_drawn_inputs = setup_inputs


def setup_inputs(seed=0):
    import zlib

    import numpy as np

    out = dict(_drawn_inputs(seed))
    spreads = {'L0_conv_bn1_gamma': (1.0, 0.2),
     'L0_conv_bn1_beta': (0.0, 0.1),
     'L0_conv_bn2_gamma': (1.0, 0.2),
     'L0_conv_bn2_beta': (0.0, 0.1),
     'L1_ffn_router_b': (0.0, 0.1),
     'L1_ffn_expert_b': (0.0, 0.1)}
    factors = {'L0_conv_w_add1': 23.725, 'L0_conv_w_add2': 3.09}
    for name, (base, spread) in spreads.items():
        noise = np.random.default_rng([zlib.crc32(name.encode()), seed]).standard_normal(out[name].shape)
        drawn = base * np.exp(spread * noise) if base else spread * noise
        out[name] = jnp.asarray(drawn.astype(out[name].dtype))
    for name, factor in factors.items():
        out[name] = (out[name] * factor).astype(out[name].dtype)
    return out
```

```python
import numpy as np
import concourse.bass as bass
from concourse import mybir
from contextlib import ExitStack

F32 = mybir.dt.float32
U32 = mybir.dt.uint32
ALU = mybir.AluOpType
ACT = mybir.ActivationFunctionType
AX = mybir.AxisListType

C = 128
H = W = 28
HP, WP = H + 2, W + 2
TAPS = 9
IMGS = 4
ROWS = H * IMGS
PIX = ROWS * W
PADDED = HP * IMGS * WP
BANKS = 7
BANK_PIX = PIX // BANKS
BANK_ROWS = ROWS // BANKS
BN_EPS = 1e-5
THRESHOLD = 0.005

GROUPS = 4
PER_GROUP = C // GROUPS
JS = 2
STEPS = PER_GROUP // JS
ACT_TAPS = 4
ACT_SLOTS, DVE_SLOTS = 5, 6
TILES = (
    "021000110101300",
    "003011020010110",
    "210100102000021",
    "000212001021001",
)
PIECE_QUAD = 0
PIECE_ROWS = ROWS // STEPS
PIECE_PIX = PIECE_ROWS * W


def plan():
    taps_done = [0] * GROUPS
    kind_done = [[0, 0] for _ in range(GROUPS)]
    quads, act, dve = [], [], []
    first, last = [len(TILES[0])] * JS, [0] * JS
    for q in range(len(TILES[0])):
        quad = []
        for g in range(GROUPS):
            p = taps_done[g] // TAPS
            k = int(TILES[g][q])
            by_act = k == 0
            start, limit = (0, ACT_TAPS) if by_act else (ACT_TAPS, TAPS)
            n = kind_done[g][by_act]
            taps = tuple(range(start + n, start + n + max(k, 1)))
            assert taps[-1] < limit
            kind_done[g][by_act] += len(taps)
            taps_done[g] += len(taps)
            if taps_done[g] % TAPS == 0:
                kind_done[g] = [0, 0]
            first[p], last[p] = min(first[p], q), max(last[p], q)
            tiles = act if by_act else dve
            quad.append((len(tiles), by_act, p))
            tiles.append((q, p, g, taps))
        quads.append(quad)
    assert taps_done == [JS * TAPS] * GROUPS
    return quads, act, dve, first, last


QUAD_PLAN, ACT_PLAN, DVE_PLAN, FIRST_QUAD, LAST_QUAD = plan()
QUADS = len(QUAD_PLAN)
ACT_TILES, DVE_TILES = len(ACT_PLAN), len(DVE_PLAN)
DVE_SUMS = sum(len(taps) - 1 for _, _, _, taps in DVE_PLAN)


def first_of(tiles, p):
    return min(n for n, tile in enumerate(tiles) if tile[1] == p)


def slot_plan(tiles, slots):
    short = -tiles % slots
    order = []
    runs = [slots] * ((tiles - short * (slots - 1)) // slots) + [slots - 1] * short
    for run in runs:
        order += list(range(run))
    before = []
    for n in range(tiles):
        m = n - 1
        while order[m % tiles] != order[n]:
            m -= 1
        before.append(m)
    return order, before


ACT_SLOT, ACT_BEFORE = slot_plan(ACT_TILES, ACT_SLOTS)
DVE_SLOT, DVE_BEFORE = slot_plan(DVE_TILES, DVE_SLOTS)


def freed_by(before, tiles):
    return tiles[before][0] + 1 if before >= 0 else tiles[before % len(tiles)][0] + 1 - QUADS


def adder_layer(nc, name, chunks, load_chunk, norm, w_shift, w_add, store, stats_out):
    ctx = ExitStack()
    with ctx:
        def sb(n, shape, dt=F32):
            return ctx.enter_context(nc.sbuf_tensor(f"{name}_{n}", shape, dt))

        def sem(n):
            return ctx.enter_context(nc.semaphore(f"{name}_{n}"))

        act_ring = sb("act_ring", [C, ACT_SLOTS, PIX])
        dve_ring = sb("dve_ring", [C, DVE_SLOTS, PIX])
        y = [sb(f"y{i}", [C, HP * IMGS, WP]) for i in range(2)]
        xin = sb("xin", [C, HP * IMGS, WP])
        box = sb("box", [C, PIX])
        wadd = sb("wadd", [C, GROUPS, PER_GROUP, TAPS])
        wq = sb("wq", [C, TAPS, C])
        w_now = sb("w_now", [C, JS, GROUPS, TAPS])
        strip = sb("strip", [C, 2, 2 * PER_GROUP - 1])
        pick = sb("pick", [C, JS, 2, PER_GROUP])
        ones = sb("ones", [C, C])
        zeros = sb("zeros", [1, C])
        wsum_taps = sb("wsum_taps", [C, C])
        wsum = sb("wsum", [C, 1])
        wraw = act_ring[:, 0, 0:TAPS * C]
        wmag = act_ring[:, 1, 0:TAPS * C]
        wpow = act_ring[:, 2, 0:TAPS * C]
        wbit = act_ring[:, 3, 0:TAPS * C]
        wflat = wq[:].rearrange("p t c -> p (t c)")

        psum = ctx.enter_context(nc.psum_tensor(f"{name}_psum", [C, 8, 512], F32))
        dist = psum[:, 0:BANKS, 0:BANK_PIX]
        piece_ps = psum[:, BANKS, 0:PIECE_PIX]

        weights_in = sem("weights_in")
        input_in = sem("input_in")
        normed = sem("normed")
        cleared = sem("cleared")
        wstep = sem("wstep")
        wsum_done = sem("wsum_done")
        piece_done = sem("piece_done")
        piece_kept = sem("piece_kept")
        staged = sem("staged")
        act_tiles = sem("act_tiles")
        dve_tiles = sem("dve_tiles")
        dve_base = sem("dve_base")
        quads_done = sem("quads_done")
        boxed = sem("boxed")
        sums_done = sem("sums_done")
        act_kept = sem("act_kept")
        dve_kept = sem("dve_kept")
        counted = sem("counted")
        stored = sem("stored")
        passed = sem("passed")

        N_ACT_BANKS = (BANKS + 1) // 2
        N_DVE_BANKS = BANKS // 2
        LOADS = load_chunk.dmas
        NORM_STEPS = 2
        BOX_STEPS = TAPS - ACT_TAPS - 1

        def window(buf, tap, row0=0, rows=ROWS):
            dy, dx = tap // 3, tap % 3
            if isinstance(row0, int):
                return buf[:, dy * IMGS + row0:dy * IMGS + row0 + rows, dx:dx + W]
            return buf[:, bass.ds(row0 + dy * IMGS, rows), dx:dx + W]

        def rows_of(flat):
            return flat.rearrange("p (r w) -> p r w", w=W)

        def inner(buf):
            return buf[:, IMGS:IMGS + ROWS, 1:1 + W]

        def over_chunks(eng, body):
            if chunks > 2:
                with eng.Fori(0, chunks // 2 - 1) as i:
                    body(i * 2, 0, True)
                    body(i * 2 + 1, 1, True)
            body(chunks - 2, 0, True)
            body(chunks - 1, 1, False)

        def over_steps(eng, first, last, step):
            with eng.Fori(first, last) as jj:
                step(jj)

        block = ctx.enter_context(nc.Block())

        @block.sync
        def _(sp):
            sp.dma_start(wraw, w_shift).then_inc(weights_in, 16)
            sp.dma_start(wadd[:].rearrange("p g j t -> p (g j t)"), w_add).then_inc(weights_in, 16)
            sp.sem_inc(stored, 16 * store.dmas)
            sp.wait_ge(cleared, 1)
            load_chunk(sp, xin, 0, input_in)
            sp.wait_ge(piece_done, BANKS)
            load_chunk(sp, xin, 1, input_in)

            def chunk_io(c, parity, last_pair):
                if not last_pair:
                    sp.wait_ge(piece_done, BANKS + (c + 1) * STEPS)
                    load_chunk(sp, xin, c + 2, input_in)
                sp.wait_ge(act_kept, (c + 2) * N_ACT_BANKS)
                sp.sem_inc(passed, 1)
                sp.wait_ge(dve_kept, (c + 2) * N_DVE_BANKS)
                store(sp, box, c, stored)

            over_chunks(sp, lambda c, parity, more: chunk_io(c, parity, isinstance(c, int)))
            sp.wait_ge(stored, 16 * store.dmas * (chunks + 1))

        @block.gpsimd
        def _(pool):
            pool.memset(xin[:], 0.0).then_inc(cleared, 1)
            pool.memset(y[0][:], 0.0).then_inc(cleared, 1)
            pool.memset(y[1][:], 0.0).then_inc(cleared, 1)
            pool.memset(ones[:], 1.0).then_inc(cleared, 1)
            pool.memset(zeros[:], 0.0).then_inc(cleared, 1)
            pool.memset(strip[:], 0.0).then_inc(cleared, 1)
            pool.wait_ge(cleared, 6)
            pool.memset(strip[:, 0, PER_GROUP - 1:PER_GROUP], -1.0).then_inc(cleared, 1)
            pool.memset(strip[:, 1, PER_GROUP - 1:PER_GROUP], -2.0).then_inc(cleared, 1)
            pool.wait_ge(cleared, 8)
            pool.wait_ge(weights_in, 32)

            def normalise(c):
                if norm is None:
                    return
                scale, shift = norm
                x = inner(xin)
                pool.wait_ge(input_in, 16 * LOADS * (c + 1))
                pool.sem_inc(passed, 1)
                pool.tensor_scalar(x, x, scale, shift, ALU.mult, ALU.add).then_inc(normed, 1)
                pool.wait_ge(normed, c * NORM_STEPS + 1)
                pool.sem_inc(passed, 1)
                pool.tensor_scalar(x, x, 0.0, None, ALU.max).then_inc(normed, 1)

            def stage(c, jj):
                for p in range(JS):
                    pool.wait_ge(quads_done, (c * STEPS + jj) * QUADS + LAST_QUAD[p] + 1)
                    pool.sem_inc(passed, 1)
                    j = jj * JS + p
                    pool.tensor_copy(w_now[:, p, :, :], wadd[:, :, bass.ds(j, 1), :].rearrange("p g o t -> p g (o t)"))\
                        .then_inc(staged, 1)
                    for s in range(2):
                        pool.tensor_copy(pick[:, p, s, :], strip[:, s, bass.ds(PER_GROUP - 1 - j, PER_GROUP)])\
                            .then_inc(staged, 1)

            def chunk_help(c, parity, more):
                stage(c, 0)
                if more:
                    normalise(c + 1)
                over_steps(pool, 1, STEPS, lambda jj: stage(c, jj))
                pool.wait_ge(piece_kept, BANKS + c * STEPS)
                pool.wait_ge(stored, 16 * store.dmas * (c + 1))
                pool.wait_ge(counted, BANKS * (c + 1))
                src = window(y[parity], ACT_TAPS)
                for n in range(BOX_STEPS):
                    if n:
                        pool.wait_ge(boxed, c * BOX_STEPS + n)
                        src = rows_of(box[:, :])
                    pool.tensor_tensor(rows_of(box[:, :]), src, window(y[parity], ACT_TAPS + 1 + n), ALU.add)\
                        .then_inc(boxed, 1)

            normalise(0)
            over_chunks(pool, chunk_help)

        @block.vector
        def _(dve):
            dve.sem_inc(dve_kept, N_DVE_BANKS)
            dve.sem_inc(counted, BANKS)
            n = [0]

            def link(ins):
                n[0] += 1
                ins.then_inc(wstep, 1)
                dve.wait_ge(wstep, n[0])

            dve.wait_ge(weights_in, 32)
            link(dve.tensor_scalar(wmag.bitcast(U32), wraw.bitcast(U32), 0x7FFFFFFF, None, ALU.bitwise_and))
            link(dve.tensor_scalar(wpow.bitcast(U32), wraw.bitcast(U32), 0x7F800000, None, ALU.bitwise_and))
            link(dve.scalar_tensor_tensor(wbit, wpow, float(np.sqrt(np.float32(2))), wmag, ALU.mult, ALU.is_lt))
            link(dve.scalar_tensor_tensor(wpow, wbit, 1.0, wpow, ALU.add, ALU.mult))
            link(dve.scalar_tensor_tensor(wpow, wmag, THRESHOLD, wpow, ALU.is_ge, ALU.mult))
            link(dve.tensor_scalar(wbit.bitcast(U32), wraw.bitcast(U32), 0x80000000, None, ALU.bitwise_and))
            link(dve.tensor_tensor(wpow.bitcast(U32), wpow.bitcast(U32), wbit.bitcast(U32), ALU.bitwise_or))
            link(dve.tensor_tensor(wpow, wpow, wraw, ALU.subtract))
            link(dve.tensor_tensor(wflat, wraw, wpow, ALU.add))
            link(dve.tensor_reduce(wsum_taps[:, :], wadd[:, :, :, ACT_TAPS:TAPS].rearrange("p g j t -> p (g j) t"),
                                   axis=AX.X, op=ALU.add))
            dve.wait_ge(wsum_done, 1)
            link(dve.tensor_copy(wsum[:, :], psum[:, BANKS, 0:1]))
            dve.wait_ge(cleared, 8)

            for b in range(BANKS):
                dve.wait_ge(piece_done, b + 1)
                dve.tensor_copy(y[0][:, IMGS + b * BANK_ROWS:IMGS + (b + 1) * BANK_ROWS, 1:1 + W], rows_of(dist[:, b, :]))\
                    .then_inc(piece_kept, 1)

            def body(c, parity, more, jj):
                u = c * STEPS + jj
                sums = 0
                for t, (q, p, g, taps) in enumerate(DVE_PLAN):
                    tile = rows_of(dve_ring[:, DVE_SLOT[t], :])
                    if t == first_of(DVE_PLAN, p):
                        dve.wait_ge(staged, u * (3 * JS) + 3 * (p + 1))
                    dve.wait_ge(quads_done, u * QUADS + QUADS + freed_by(DVE_BEFORE[t], DVE_PLAN))
                    tap = taps[0]
                    ins = dve.tensor_scalar(tile, window(y[parity], tap), w_now[:, p, g, tap:tap + 1], None, ALU.max)
                    for tap in taps[1:]:
                        ins.then_inc(dve_base, 1)
                        sums += 1
                        dve.wait_ge(dve_base, u * DVE_SUMS + sums)
                        ins = dve.scalar_tensor_tensor(tile, window(y[parity], tap), w_now[:, p, g, tap:tap + 1], tile,
                                                       ALU.max, ALU.add)
                    ins.then_inc(dve_tiles, 1)
                if more:
                    dve.wait_ge(piece_done, BANKS + u + 1)
                    dve.tensor_copy(y[1 - parity][:, bass.ds(jj * PIECE_ROWS + IMGS, PIECE_ROWS), 1:1 + W],
                                    rows_of(piece_ps)).then_inc(piece_kept, 1)

            def chunk_work(c, parity, more):
                dve.wait_ge(piece_kept, BANKS + c * STEPS)
                dve.sem_inc(passed, 1)
                over_steps(dve, 0, STEPS, lambda jj: body(c, parity, more, jj))
                for b in range(1, BANKS, 2):
                    dve.wait_ge(sums_done, c * BANKS + b + 1)
                    dve.tensor_scalar(box[:, b * BANK_PIX:(b + 1) * BANK_PIX], dist[:, b, :], wsum[:, 0:1], None, ALU.add)\
                        .then_inc(dve_kept, 1)
                for b in range(BANKS):
                    if b % 2:
                        dve.wait_ge(dve_kept, (c + 1) * N_DVE_BANKS + b // 2 + 1)
                    else:
                        dve.wait_ge(act_kept, (c + 1) * N_ACT_BANKS + b // 2 + 1)
                    dve.bn_stats(stats_out[:, bass.ds(c * BANKS + b, 1), :].rearrange("p o s -> p (o s)"),
                                 box[:, b * BANK_PIX:(b + 1) * BANK_PIX]).then_inc(counted, 1)

            over_chunks(dve, chunk_work)

        @block.scalar
        def _(act):
            def body(c, parity, jj):
                u = c * STEPS + jj
                for t, (q, p, g, (tap,)) in enumerate(ACT_PLAN):
                    if t == first_of(ACT_PLAN, p):
                        act.wait_ge(staged, u * (3 * JS) + 3 * (p + 1))
                    act.wait_ge(quads_done, u * QUADS + QUADS + freed_by(ACT_BEFORE[t], ACT_PLAN))
                    act.activation(rows_of(act_ring[:, ACT_SLOT[t], :]), window(y[parity], tap), ACT.Abs,
                                   bias=w_now[:, p, g, tap:tap + 1], scale=-1.0).then_inc(act_tiles, 1)

            def chunk_work(c, parity, more):
                act.wait_ge(piece_kept, BANKS + c * STEPS)
                act.sem_inc(passed, 1)
                over_steps(act, 0, STEPS, lambda jj: body(c, parity, jj))
                for b in range(0, BANKS, 2):
                    act.wait_ge(sums_done, c * BANKS + b + 1)
                    act.activation(box[:, b * BANK_PIX:(b + 1) * BANK_PIX], dist[:, b, :], ACT.Identity,
                                   bias=wsum[:, 0:1], scale=1.0).then_inc(act_kept, 1)

            act.sem_inc(act_kept, N_ACT_BANKS)
            act.preload_act_table(ACT.Abs)
            act.wait_ge(wstep, 11)
            over_chunks(act, chunk_work)

        @block.tensor
        def _(pe):
            pe.sem_inc(quads_done, QUADS)
            pe.wait_ge(cleared, 8)
            pe.wait_ge(wstep, 10)
            pe.matmul(psum[:, BANKS, 0:1], wsum_taps[:, :], ones[:, 0:1], start=True, stop=True).then_inc(wsum_done, 1)
            pe.wait_ge(wstep, 11)

            def piece(ps, row0, rows):
                for tap in range(TAPS):
                    last = pe.matmul(rows_of(ps), wq[:, tap, :], window(xin, tap, row0, rows),
                                     start=(tap == 0), stop=(tap == TAPS - 1))
                last.then_inc(piece_done, 1)

            def input_ready(c):
                if norm is None:
                    pe.wait_ge(input_in, 16 * LOADS * (c + 1))
                else:
                    pe.wait_ge(normed, NORM_STEPS * (c + 1))

            input_ready(0)
            for b in range(BANKS):
                piece(dist[:, b, :], b * BANK_ROWS, BANK_ROWS)

            def body(c, parity, more, jj):
                u = c * STEPS + jj
                for q, quad in enumerate(QUAD_PLAN):
                    if q == PIECE_QUAD and more:
                        input_ready(c + 1)
                        pe.wait_ge(piece_kept, BANKS + u)
                        piece(piece_ps, jj * PIECE_ROWS, PIECE_ROWS)
                    for p in range(JS):
                        if q == FIRST_QUAD[p]:
                            pe.wait_ge(staged, u * (3 * JS) + 3 * (p + 1))
                    pe.wait_ge(act_tiles, u * ACT_TILES + sum(t[0] <= q for t in ACT_PLAN))
                    pe.wait_ge(dve_tiles, u * DVE_TILES + sum(t[0] <= q for t in DVE_PLAN))
                    for b in range(BANKS):
                        for g, (t, is_act, p) in enumerate(quad):
                            tile = act_ring[:, ACT_SLOT[t], :] if is_act else dve_ring[:, DVE_SLOT[t], :]
                            last = pe.matmul(dist[PER_GROUP * g:PER_GROUP * (g + 1), b, :],
                                             pick[:, p, 0 if is_act else 1, :],
                                             tile[:, b * BANK_PIX:(b + 1) * BANK_PIX], start=False, stop=False,
                                             skip_group_check=True)
                    last.then_inc(quads_done, 1)

            def chunk_work(c, parity, more):
                pe.wait_ge(piece_kept, BANKS + c * STEPS)
                for b in range(BANKS):
                    if b % 2:
                        pe.wait_ge(dve_kept, c * N_DVE_BANKS + b // 2 + 1)
                    else:
                        pe.wait_ge(act_kept, c * N_ACT_BANKS + b // 2 + 1)
                    pe.matmul(dist[:, b, 0:1], zeros[:, :], ones[0:1, 0:1], start=True, stop=False,
                              skip_group_check=True)
                over_steps(pe, 0, STEPS, lambda jj: body(c, parity, more, jj))
                pe.wait_ge(boxed, c * BOX_STEPS + BOX_STEPS)
                for b in range(BANKS):
                    pe.matmul(dist[:, b, :], ones[:, :], box[:, b * BANK_PIX:(b + 1) * BANK_PIX], start=False,
                              stop=True, skip_group_check=True).then_inc(sums_done, 1)

            over_chunks(pe, chunk_work)


TOK = H * W
TT = 112
NT = TOK // TT
PER_BANK = 4
SPLIT = PER_BANK * TT
E = 8
V1 = C + 1
O_BANK = 3
LN_EPS = 1e-5
DEN_EPS = 1e-6


def batch_norm_scale(nc, name, stats, gamma, beta, scale, shift):
    with (
        nc.sbuf_tensor(f"{name}_mv", [C, 2], F32) as mv,
        nc.sbuf_tensor(f"{name}_gb", [C, 2], F32) as gb,
        nc.sbuf_tensor(f"{name}_half", [C, 1], F32) as half,
        nc.sbuf_tensor(f"{name}_rstd", [C, 1], F32) as rstd,
        nc.semaphore(f"{name}_params_in") as params_in,
        nc.semaphore(f"{name}_mv_ready") as mv_ready,
        nc.semaphore(f"{name}_half_ready") as half_ready,
        nc.semaphore(f"{name}_rstd_ready") as rstd_ready,
        nc.semaphore(f"{name}_scaled") as scaled,
        nc.Block() as block,
    ):
        @block.sync
        def _(sp):
            sp.dma_start(gb[:, 0:1], gamma).then_inc(params_in, 16)
            sp.dma_start(gb[:, 1:2], beta).then_inc(params_in, 16)

        @block.gpsimd
        def _(pool):
            pool.memset(half[:], -0.5).then_inc(half_ready, 1)
            pool.wait_ge(half_ready, 1)
            pool.wait_ge(mv_ready, 2)
            pool.tensor_tensor(rstd[:], mv[:, 1:2], half[:], ALU.pow).then_inc(rstd_ready, 1)

        @block.vector
        def _(dve):
            dve.bn_aggr(mv[:], stats[:].rearrange("p n s -> p (n s)")).then_inc(mv_ready, 1)
            dve.wait_ge(mv_ready, 1)
            dve.tensor_scalar(mv[:, 1:2], mv[:, 1:2], BN_EPS, None, ALU.add).then_inc(mv_ready, 1)
            dve.wait_ge(rstd_ready, 1)
            dve.wait_ge(params_in, 32)
            dve.tensor_tensor(scale, gb[:, 0:1], rstd[:], ALU.mult).then_inc(scaled, 1)
            dve.wait_ge(scaled, 1)
            dve.tensor_tensor(shift, mv[:, 0:1], scale, ALU.mult).then_inc(scaled, 1)
            dve.wait_ge(scaled, 2)
            dve.tensor_tensor(shift, gb[:, 1:2], shift, ALU.subtract).then_inc(scaled, 1)


def token_layer(nc, images, conv_image, x_image, scale, shift, wqkv, b_qkv, b_v, router_w, router_b,
                expert_w, expert_b, out_image):
    ctx = ExitStack()
    with ctx:
        def sb(n, shape, dt=F32):
            return ctx.enter_context(nc.sbuf_tensor(f"t_{n}", shape, dt))

        def sem(n):
            return ctx.enter_context(nc.semaphore(f"t_{n}"))

        ident = sb("ident", [C, C])
        causal = sb("causal", [TT, TT])
        minus_half = sb("minus_half", [TT, NT])
        rank = sb("rank", [TT, E])
        w_qkv = sb("w_qkv", [C, 3, C])
        bias_qk = sb("bias_qk", [C, 3])
        bias_qk1 = sb("bias_qk1", [C, 3])
        bias_v = sb("bias_v", [TT, C])
        w_router = sb("w_router", [C, E])
        bias_router = sb("bias_router", [TT, E])
        w_expert = sb("w_expert", [C, E * C])
        bias_expert = sb("bias_expert", [NT * E, NT * C])

        conv_in = sb("conv_in", [C, TOK])
        x_in = sb("x_in", [C, TOK])
        pre = sb("pre", [C, TOK])
        t_ch = sb("t_ch", [C, TOK])
        t_tok = sb("t_tok", [TT, NT, C])
        st_a = sb("st_a", [TT, NT, 6])
        mv_a = sb("mv_a", [TT, NT, 2])
        var_a = sb("var_a", [TT, NT])
        rstd_a = sb("rstd_a", [TT, NT])
        norm_a = sb("norm_a", [TT, NT, C])
        norm_a_ch = sb("norm_a_ch", [C, TOK])
        low = [sb(f"low_{s}", [C, TOK]) for s in "qk"]
        qk = [sb(f"{s}_ch", [C, TOK]) for s in "qk"]
        q_ch, k_ch = qk
        k_tok = sb("k_tok", [TT, NT, C])
        v_tok = sb("v_tok", [TT, NT, V1])
        score = sb("score", [TT, NT, TT])
        state = sb("state", [C, NT, V1])
        den = sb("den", [TT, 9])
        rden = sb("rden", [TT, NT])
        t2 = sb("t2", [TT, NT, C])

        st_b = sb("st_b", [TT, NT, 6])
        mv_b = sb("mv_b", [TT, NT, 2])
        var_b = sb("var_b", [TT, NT])
        rstd_b = sb("rstd_b", [TT, NT])
        norm_b = sb("norm_b", [TT, NT, C])
        norm_b_ch = sb("norm_b_ch", [C, TOK])
        prob = sb("prob", [TT, NT, E])
        work = sb("work", [TT, NT, E])
        mask1 = sb("mask1", [TT, NT, E])
        mask2 = sb("mask2", [TT, NT, E])
        top = sb("top", [TT, 4, NT])
        gate = sb("gate", [TT, NT, E])
        gate_t = sb("gate_t", [NT * E, TT])
        t3 = sb("t3", [TT, NT, C])
        out_ch = sb("out_ch", [C, TOK])

        psum = ctx.enter_context(nc.psum_tensor("t_psum", [C, 8, 512], F32))

        def by_channels(bank):
            return [(slice(0, SPLIT), psum[:, bank, 0:SPLIT]), (slice(SPLIT, TOK), psum[:, bank + 1, 0:TOK - SPLIT])]

        def ch_tile(bank, t):
            return psum[:, bank + t // PER_BANK, (t % PER_BANK) * TT:(t % PER_BANK + 1) * TT]

        def by_tokens(bank):
            return psum[0:TT, bank:bank + 2, :].rearrange("p b (t c) -> p (b t) c", c=C)[:, 0:NT, :]

        def tok_tile(bank, t):
            return psum[0:TT, bank + t // PER_BANK, (t % PER_BANK) * C:(t % PER_BANK + 1) * C]

        def score_tile(t):
            return psum[0:TT, t // PER_BANK, (t % PER_BANK) * TT:(t % PER_BANK + 1) * TT]

        def state_tile(t):
            return psum[:, 2 + t // O_BANK, (t % O_BANK) * V1:(t % O_BANK + 1) * V1]

        def o_tile(t):
            return psum[0:TT, t // O_BANK, (t % O_BANK) * V1:(t % O_BANK + 1) * V1]

        def cols(t):
            return slice(t * TT, (t + 1) * TT)

        T01, B23, EXPERTS, B67 = 0, 2, 4, 6
        logits_ps = psum[0:TT, B67, 0:NT * E].rearrange("p (t e) -> p t e", e=E)
        gate_ps = psum[0:NT * E, B67 + 1, 0:TT]

        consts_in = sem("consts_in")
        const_made = sem("const_made")
        const_sum = sem("const_sum")
        loaded = sem("loaded")
        pre_ready = sem("pre_ready")
        t_ch_ready = sem("t_ch_ready")
        t_ps = sem("t_ps")
        t_tok_ready = sem("t_tok_ready")
        stat_a = sem("stat_a")
        var_a_made = sem("var_a_made")
        rstd_a_ready = sem("rstd_a_ready")
        norm_a_ready = sem("norm_a_ready")
        norm_a_ps = sem("norm_a_ps")
        norm_a_ch_ready = sem("norm_a_ch_ready")
        qk_ps = sem("qk_ps")
        low_ready = sem("low_ready")
        exp_ready = sem("exp_ready")
        qk_ready = sem("qk_ready")
        v_ps = sem("v_ps")
        v_ready = sem("v_ready")
        k_ps = sem("k_ps")
        k_tok_ready = sem("k_tok_ready")
        score_ps = sem("score_ps")
        score_ready = sem("score_ready")
        state_ps = sem("state_ps")
        state_step = sem("state_step")
        o_ps = sem("o_ps")
        den_step = sem("den_step")
        t2_ready = sem("t2_ready")
        stat_b = sem("stat_b")
        var_b_made = sem("var_b_made")
        rstd_b_ready = sem("rstd_b_ready")
        norm_b_ready = sem("norm_b_ready")
        norm_b_ps = sem("norm_b_ps")
        norm_b_ch_ready = sem("norm_b_ch_ready")
        logits_made = sem("logits_made")
        gate_step = sem("gate_step")
        prob_exp = sem("prob_exp")
        gate_t_made = sem("gate_t_made")
        gate_t_ready = sem("gate_t_ready")
        bias_made = sem("bias_made")
        expert_made = sem("expert_made")
        acc_step = sem("acc_step")
        out_ps = sem("out_ps")
        out_ch_ready = sem("out_ch_ready")
        out_stored = sem("out_stored")
        passed = sem("passed")
        GATE_STEPS = 24
        ACC_STEPS = NT * (E + 1)

        def pipelined(eng, attention_first, both, experts_last):
            attention_first(0)
            with eng.Fori(0, images - 1) as i:
                both(i + 1, i)
            experts_last(images - 1)

        block = ctx.enter_context(nc.Block())

        @block.sync
        def _(sp):
            def load(n):
                sp.dma_start(conv_in[:, :], conv_image(n)).then_inc(loaded, 16)
                sp.dma_start(x_in[:, :], x_image(n)).then_inc(loaded, 16)

            def keep(n):
                sp.wait_ge(out_ch_ready, n + 2)
                sp.dma_start(out_image(n), out_ch[:, :]).then_inc(out_stored, 16)

            sp.sem_inc(out_stored, 16)
            load(0)
            sp.dma_start(w_qkv[:].rearrange("p s c -> p (s c)"), wqkv).then_inc(consts_in, 16)
            sp.dma_start(bias_qk[:, :], b_qkv).then_inc(consts_in, 16)
            sp.dma_start(bias_v[:, :], b_v).then_inc(consts_in, 16)
            sp.dma_start(w_router[:, :], router_w).then_inc(consts_in, 16)
            sp.dma_start(bias_router[:, :], router_b).then_inc(consts_in, 16)
            sp.dma_start(w_expert[:, :], expert_w).then_inc(consts_in, 16)
            sp.wait_ge(const_made, 8)
            for t in range(NT):
                sp.dma_start(bias_expert[t * E:(t + 1) * E, t * C:(t + 1) * C], expert_b).then_inc(consts_in, 16)
            sp.wait_ge(pre_ready, 1)
            load(1)
            if images > 2:
                with sp.Fori(0, images - 2) as i:
                    sp.wait_ge(pre_ready, i + 2)
                    load(i + 2)
                    keep(i)
            keep(images - 2)
            keep(images - 1)
            sp.wait_ge(out_stored, 16 * (images + 1))

        CONSTS = 16 * (6 + NT)

        @block.gpsimd
        def _(pool):
            pool.memset(ident[:], 0.0).then_inc(const_made, 1)
            pool.memset(causal[:], 1.0).then_inc(const_made, 1)
            pool.memset(minus_half[:], -0.5).then_inc(const_made, 1)
            pool.memset(bias_expert[:], 0.0).then_inc(const_made, 1)
            pool.memset(v_tok[:, :, C:V1], 1.0).then_inc(const_made, 1)
            pool.memset(rank[:], 1.0).then_inc(const_made, 1)
            pool.wait_ge(const_made, 6)
            pool.affine_select(out=ident[:], in_=ident[:], compare_op=ALU.not_equal, fill=1.0, base=0,
                               pattern=[[-1, C]], channel_multiplier=1).then_inc(const_made, 1)
            pool.affine_select(out=causal[:], in_=causal[:], compare_op=ALU.is_ge, fill=0.0, base=0,
                               pattern=[[1, TT]], channel_multiplier=-1).then_inc(const_made, 1)
            for e in range(E - 1):
                pool.memset(rank[:, e:e + 1], float(E - e)).then_inc(const_made, 1)

            def rstd(n, stat, mv, var, var_made, out, ready):
                pool.wait_ge(stat, 2 * NT * (n + 1))
                pool.sem_inc(passed, 1)
                pool.tensor_scalar(var[:], mv[:, :, 1], LN_EPS, None, ALU.add).then_inc(var_made, 1)
                pool.wait_ge(var_made, n + 1)
                pool.tensor_tensor(out[:], var[:], minus_half[:], ALU.pow).then_inc(ready, 1)

            def rstd_of_a(n):
                rstd(n, stat_a, mv_a, var_a, var_a_made, rstd_a, rstd_a_ready)

            def rstd_of_b(n):
                rstd(n, stat_b, mv_b, var_b, var_b_made, rstd_b, rstd_b_ready)

            def both(a, b):
                rstd_of_b(b)
                rstd_of_a(a)

            pipelined(pool, rstd_of_a, both, rstd_of_b)

        @block.vector
        def _(dve):
            def a_pre(n):
                dve.wait_ge(loaded, 32 * (n + 1))
                dve.scalar_tensor_tensor(pre[:, :], conv_in[:, :], scale, x_in[:, :], ALU.mult, ALU.add)\
                    .then_inc(pre_ready, 1)

            def stats(n, src, st, mv, stat):
                for t in range(NT):
                    dve.bn_stats(st[:, t, :], src[:, t, :]).then_inc(stat, 1)
                for t in range(NT):
                    if t == 0:
                        dve.wait_ge(stat, 2 * NT * n + NT)
                        dve.sem_inc(passed, 1)
                    dve.bn_aggr(mv[:, t, :], st[:, t, :]).then_inc(stat, 1)

            def normalise(src, mv, rstd, out, ready):
                for t in range(NT):
                    last = dve.tensor_scalar(out[:, t, :], src[:, t, :], mv[:, t, 0:1], rstd[:, t:t + 1],
                                             ALU.subtract, ALU.mult)
                last.then_inc(ready, 1)

            def a_stats(n):
                dve.wait_ge(t_tok_ready, n + 1)
                stats(n, t_tok, st_a, mv_a, stat_a)

            def a_norm(n):
                dve.wait_ge(rstd_a_ready, n + 1)
                normalise(t_tok, mv_a, rstd_a, norm_a, norm_a_ready)

            def a_low(n):
                for s, bank in ((0, T01), (1, B23)):
                    dve.wait_ge(qk_ps, 2 * n + s + 1)
                    for at, ps in by_channels(bank):
                        last = dve.tensor_scalar(low[s][:, at], ps, bias_qk[:, s:s + 1], 0.0, ALU.add, ALU.min)
                    last.then_inc(low_ready, 1)

            def a_elu(n):
                for s, bank in ((0, T01), (1, B23)):
                    dve.wait_ge(exp_ready, 2 * n + s + 1)
                    for at, ps in by_channels(bank):
                        last = dve.scalar_tensor_tensor(qk[s][:, at], ps, bias_qk1[:, s:s + 1], low[s][:, at],
                                                        ALU.add, ALU.max)
                    last.then_inc(qk_ready, 1)

            def a_v(n):
                dve.wait_ge(v_ps, n + 1)
                dve.tensor_tensor(v_tok[:, :, 0:C], by_tokens(T01),
                                  bias_v[:, :].rearrange("p (o c) -> p o c", o=1).broadcast_to((TT, NT, C)), ALU.add)\
                    .then_inc(v_ready, 1)

            def a_scores(n):
                dve.wait_ge(score_ps, n + 1)
                mask = causal[:, :].rearrange("p (o c) -> p o c", o=1)
                for t, k in ((0, PER_BANK), (PER_BANK, NT - PER_BANK)):
                    last = dve.tensor_tensor(score[:, t:t + k, :],
                                             psum[0:TT, t // PER_BANK, 0:k * TT].rearrange("p (t c) -> p t c", c=TT),
                                             mask.broadcast_to((TT, k, TT)), ALU.mult)
                last.then_inc(score_ready, 1)

            def a_state(n):
                dve.wait_ge(state_ps, n + 1)
                dve.tensor_copy(state[:, 1, :], state_tile(0)).then_inc(state_step, 1)
                for t in range(2, NT):
                    dve.wait_ge(state_step, (NT - 1) * n + t - 1)
                    dve.tensor_tensor(state[:, t, :], state_tile(t - 1), state[:, t - 1, :], ALU.add)\
                        .then_inc(state_step, 1)

            def a_out(n):
                dve.wait_ge(o_ps, n + 1)
                full = psum[0:TT, 0:2, 0:O_BANK * V1].rearrange("p b (t c) -> p b t c", c=V1)[:, :, :, C:V1]
                dve.tensor_scalar(den[:, 0:6].rearrange("p (b t o) -> p b t o", b=2, o=1), full, DEN_EPS, None, ALU.add)\
                    .then_inc(den_step, 1)
                dve.tensor_scalar(den[:, 6:7], o_tile(6)[:, C:V1], DEN_EPS, None, ALU.add).then_inc(den_step, 1)
                dve.wait_ge(den_step, 3 * n + 2)
                dve.reciprocal(rden[:, :], den[:, 0:NT]).then_inc(den_step, 1)
                dve.wait_ge(den_step, 3 * n + 3)
                for t in range(NT):
                    last = dve.scalar_tensor_tensor(t2[:, t, :], o_tile(t)[:, 0:C], rden[:, t:t + 1], t_tok[:, t, :],
                                                    ALU.mult, ALU.add)
                last.then_inc(t2_ready, 1)

            def b_stats(n):
                dve.wait_ge(t2_ready, n + 1)
                stats(n, t2, st_b, mv_b, stat_b)

            def b_norm(n):
                dve.wait_ge(rstd_b_ready, n + 1)
                normalise(t2, mv_b, rstd_b, norm_b, norm_b_ready)

            def b_router(n):
                at = [0]

                def step(ins):
                    at[0] += 1
                    ins.then_inc(gate_step, 1)
                    dve.wait_ge(gate_step, GATE_STEPS * n + at[0])

                def per_expert(x):
                    return x.rearrange("p (t o) -> p t o", o=1).broadcast_to((TT, NT, E))

                ranks = rank[:, :].rearrange("p (o e) -> p o e", o=1).broadcast_to((TT, NT, E))
                biases = bias_router[:, :].rearrange("p (o e) -> p o e", o=1).broadcast_to((TT, NT, E))
                some, first, second, total = (top[:, i, :] for i in range(4))

                def highest(out, x):
                    step(dve.tensor_reduce(out, x[:, :, :], axis=AX.X, op=ALU.max))

                dve.wait_ge(logits_made, n + 1)
                step(dve.tensor_tensor(prob[:, :, :], logits_ps, biases, ALU.add))
                highest(some, prob)
                step(dve.tensor_tensor(prob[:, :, :], prob[:, :, :], per_expert(some), ALU.subtract))
                dve.wait_ge(prob_exp, n + 1)
                step(dve.tensor_reduce(total, prob[:, :, :], axis=AX.X, op=ALU.add))
                step(dve.reciprocal(total, total))
                step(dve.tensor_tensor(prob[:, :, :], prob[:, :, :], per_expert(total), ALU.mult))
                for value, mask in ((first, mask1), (second, mask2)):
                    highest(value, prob)
                    step(dve.tensor_tensor(work[:, :, :], prob[:, :, :], per_expert(value), ALU.is_equal))
                    step(dve.tensor_tensor(work[:, :, :], work[:, :, :], ranks, ALU.mult))
                    highest(some, work)
                    step(dve.tensor_tensor(mask[:, :, :], work[:, :, :], per_expert(some), ALU.is_equal))
                    if mask is mask1:
                        step(dve.scalar_tensor_tensor(prob[:, :, :], mask[:, :, :], -2.0, prob[:, :, :], ALU.mult, ALU.add))
                step(dve.tensor_tensor(total, first, second, ALU.add))
                step(dve.reciprocal(total, total))
                step(dve.tensor_tensor(first, first, total, ALU.mult))
                step(dve.tensor_tensor(second, second, total, ALU.mult))
                step(dve.tensor_tensor(gate[:, :, :], mask1[:, :, :], per_expert(first), ALU.mult))
                step(dve.tensor_tensor(work[:, :, :], mask2[:, :, :], per_expert(second), ALU.mult))
                step(dve.tensor_tensor(gate[:, :, :], gate[:, :, :], work[:, :, :], ALU.add))
                assert at[0] == GATE_STEPS

            def b_tile(n, t):
                for e in range(E):
                    if e % PER_BANK == 0:
                        dve.wait_ge(expert_made, 2 * NT * n + 2 * t + e // PER_BANK + 1)
                    if e:
                        dve.wait_ge(acc_step, ACC_STEPS * n + (E + 1) * (t + 1) + e)
                    src = t3 if e else t2
                    dve.scalar_tensor_tensor(
                        t3[:, t, :], psum[0:TT, EXPERTS + e // PER_BANK, (e % PER_BANK) * C:(e % PER_BANK + 1) * C],
                        gate[:, t, e:e + 1], src[:, t, :], ALU.mult, ALU.add).then_inc(acc_step, 1)
                dve.wait_ge(acc_step, ACC_STEPS * n + (E + 1) * (t + 1) + E)
                if t == 0:
                    dve.wait_ge(bias_made, n + 1)
                dve.tensor_tensor(t3[:, t, :], tok_tile(B67, t), t3[:, t, :], ALU.add).then_inc(acc_step, 1)

            def attention(n):
                a_pre(n)
                a_stats(n)
                a_norm(n)
                a_low(n)
                a_elu(n)
                a_v(n)
                a_scores(n)
                a_state(n)
                a_out(n)

            def both(a, b):
                a_pre(a)
                b_stats(b)
                a_stats(a)
                b_norm(b)
                a_norm(a)
                b_router(b)
                a_low(a)
                b_tile(b, 0)
                a_elu(a)
                a_v(a)
                b_tile(b, 1)
                a_scores(a)
                a_state(a)
                for t in range(2, NT):
                    b_tile(b, t)
                a_out(a)

            def experts(n):
                b_stats(n)
                b_norm(n)
                b_router(n)
                for t in range(NT):
                    b_tile(n, t)

            dve.sem_inc(acc_step, E + 1)
            dve.wait_ge(consts_in, CONSTS)
            dve.wait_ge(const_made, 8 + E - 1)
            dve.tensor_scalar(bias_qk1[:, :], bias_qk[:, :], 1.0, None, ALU.add).then_inc(const_sum, 1)
            dve.wait_ge(const_sum, 1)
            pipelined(dve, attention, both, experts)

        @block.scalar
        def _(act):
            def a_relu(n):
                act.wait_ge(pre_ready, n + 1)
                act.activation(t_ch[:, :], pre[:, :], ACT.Relu, bias=shift, scale=1.0).then_inc(t_ch_ready, 1)

            def a_t_tok(n):
                act.wait_ge(t_ps, n + 1)
                act.copy(t_tok[:, :, :], by_tokens(T01)).then_inc(t_tok_ready, 1)

            def keep_channels(out, bank, made, at_least, ready):
                act.wait_ge(made, at_least)
                for at, ps in by_channels(bank):
                    last = act.copy(out[:, at], ps)
                last.then_inc(ready, 1)

            def a_norm(n):
                keep_channels(norm_a_ch, B23, norm_a_ps, n + 1, norm_a_ch_ready)

            def a_exp(n):
                for s in range(2):
                    act.wait_ge(low_ready, 2 * n + s + 1)
                    act.activation(low[s][:, :], low[s][:, :], ACT.Exp).then_inc(exp_ready, 1)

            def a_k(n):
                act.wait_ge(k_ps, n + 1)
                act.copy(k_tok[:, :, :], by_tokens(B23)).then_inc(k_tok_ready, 1)

            def b_norm(n):
                keep_channels(norm_b_ch, B67, norm_b_ps, n + 1, norm_b_ch_ready)

            def b_prob(n):
                act.wait_ge(gate_step, GATE_STEPS * n + 3)
                act.activation(prob[:, :, :], prob[:, :, :], ACT.Exp).then_inc(prob_exp, 1)

            def b_gate(n):
                act.wait_ge(gate_t_made, n + 1)
                act.copy(gate_t[:, :], gate_ps).then_inc(gate_t_ready, 1)

            def b_out(n):
                act.wait_ge(out_stored, 16 * (n + 1))
                keep_channels(out_ch, B67, out_ps, n + 1, out_ch_ready)

            def attention(n):
                a_relu(n)
                a_t_tok(n)
                a_norm(n)
                a_exp(n)
                a_k(n)

            def both(a, b):
                a_relu(a)
                a_t_tok(a)
                b_norm(b)
                a_norm(a)
                b_prob(b)
                b_gate(b)
                a_exp(a)
                a_k(a)
                b_out(b)

            def experts(n):
                b_norm(n)
                b_prob(n)
                b_gate(n)
                b_out(n)

            act.sem_inc(out_ch_ready, 1)
            act.preload_act_table(ACT.Exp)
            pipelined(act, attention, both, experts)

        @block.tensor
        def _(pe):
            def to_channels(src, bank, ready, at_least, made):
                pe.wait_ge(ready, at_least)
                for t in range(NT):
                    last = pe.transpose(ch_tile(bank, t), src[:, t, :], ident[0:TT, 0:TT])
                last.then_inc(made, 1)

            def to_tokens(src, bank, made):
                for t in range(NT):
                    last = pe.transpose(tok_tile(bank, t), src[:, cols(t)], ident[:, :])
                last.then_inc(made, 1)

            def a_t(n):
                pe.wait_ge(t_ch_ready, n + 1)
                if not isinstance(n, int) or n > 0:
                    pe.wait_ge(t2_ready, n)
                to_tokens(t_ch, T01, t_ps)

            def a_norm(n):
                to_channels(norm_a, B23, norm_a_ready, n + 1, norm_a_ps)

            def a_qk(n):
                pe.wait_ge(norm_a_ch_ready, n + 1)
                for s, bank in ((0, T01), (1, B23)):
                    for at, ps in by_channels(bank):
                        last = pe.matmul(ps, w_qkv[:, s, :], norm_a_ch[:, at], start=True, stop=True)
                    last.then_inc(qk_ps, 1)

            def a_v(n):
                pe.wait_ge(qk_ready, 2 * n + 1)
                for t in range(NT):
                    last = pe.matmul(tok_tile(T01, t), norm_a_ch[:, cols(t)], w_qkv[:, 2, :], start=True, stop=True)
                last.then_inc(v_ps, 1)
                pe.wait_ge(qk_ready, 2 * n + 2)
                to_tokens(k_ch, B23, k_ps)

            def a_scores(n):
                pe.wait_ge(v_ready, n + 1)
                for t in range(NT):
                    last = pe.matmul(score_tile(t), k_ch[:, cols(t)], q_ch[:, cols(t)], start=True, stop=True)
                last.then_inc(score_ps, 1)
                pe.wait_ge(k_tok_ready, n + 1)
                for t in range(NT - 1):
                    last = pe.matmul(state_tile(t), k_tok[:, t, :], v_tok[:, t, :], start=True, stop=True)
                last.then_inc(state_ps, 1)

            def a_out(n):
                pe.wait_ge(score_ready, n + 1)
                pe.wait_ge(state_step, (NT - 1) * (n + 1))
                for t in range(NT):
                    last = pe.matmul(o_tile(t), score[:, t, :], v_tok[:, t, :], start=True, stop=(t == 0))
                    if t:
                        last = pe.matmul(o_tile(t), q_ch[:, cols(t)], state[:, t, :], start=False, stop=True)
                last.then_inc(o_ps, 1)

            def b_norm(n):
                pe.wait_ge(out_ch_ready, n + 1)
                to_channels(norm_b, B67, norm_b_ready, n + 1, norm_b_ps)

            def b_router(n):
                pe.wait_ge(norm_b_ch_ready, n + 1)
                for t in range(NT):
                    last = pe.matmul(logits_ps[:, t, :], norm_b_ch[:, cols(t)], w_router[:, :], start=True, stop=True)
                last.then_inc(logits_made, 1)

            def b_gates(n):
                pe.wait_ge(gate_step, GATE_STEPS * (n + 1))
                pe.sem_inc(passed, 1)
                pe.transpose(gate_ps, gate[:, :, :].rearrange("p t e -> p (t e)"), ident[0:TT, 0:TT]).then_inc(gate_t_made, 1)
                pe.wait_ge(gate_t_ready, n + 1)
                for b, k in ((0, PER_BANK), (1, NT - PER_BANK)):
                    last = pe.matmul(psum[0:TT, B67 + b, 0:k * C], gate_t[:, :],
                                     bias_expert[:, b * PER_BANK * C:(b * PER_BANK + k) * C], start=True, stop=True)
                last.then_inc(bias_made, 1)

            def b_experts(n, t):
                for half in range(2):
                    pe.wait_ge(acc_step, ACC_STEPS * n + (E + 1) * t + PER_BANK * (half + 1))
                    pe.matmul(psum[0:TT, EXPERTS + half, :], norm_b_ch[:, cols(t)],
                              w_expert[:, half * PER_BANK * C:(half + 1) * PER_BANK * C], start=True, stop=True)                        .then_inc(expert_made, 1)

            def b_out(n):
                to_channels(t3, B67, acc_step, ACC_STEPS * (n + 1) + E + 1, out_ps)

            def attention(n):
                a_t(n)
                a_norm(n)
                a_qk(n)
                a_v(n)
                a_scores(n)
                a_out(n)

            def both(a, b):
                a_t(a)
                b_norm(b)
                a_norm(a)
                b_router(b)
                a_qk(a)
                b_gates(b)
                b_experts(b, 0)
                a_v(a)
                b_experts(b, 1)
                a_scores(a)
                b_experts(b, 2)
                b_experts(b, 3)
                a_out(a)
                for t in range(4, NT):
                    b_experts(b, t)
                b_out(b)

            def experts(n):
                b_norm(n)
                b_router(n)
                b_gates(n)
                for t in range(NT):
                    b_experts(n, t)
                b_out(n)

            pe.wait_ge(consts_in, CONSTS)
            pe.wait_ge(const_made, 8 + E - 1)
            pipelined(pe, attention, both, experts)


class ImageLoads:
    dmas = IMGS

    def __init__(self, x):
        self.x = x

    def __call__(self, sp, xin, chunk, done):
        view = xin[:].rearrange("p (h n) w -> p h n w", n=IMGS)
        for n in range(IMGS):
            sp.dma_start(view[:, 1:1 + H, n, 1:1 + W],
                         self.x[bass.ds(chunk * IMGS + n, 1)].rearrange("o c h w -> (o c) h w")).then_inc(done, 16)


class ChunkLoad:
    dmas = 1

    def __init__(self, kept):
        self.kept = kept

    def __call__(self, sp, xin, chunk, done):
        sp.dma_start(xin[:, IMGS:IMGS + ROWS, 1:1 + W],
                     self.kept[bass.ds(chunk, 1)].rearrange("o c (r w) -> (o c) r w", w=W)).then_inc(done, 16)


class ChunkStore:
    dmas = 1

    def __init__(self, kept):
        self.kept = kept

    def __call__(self, sp, box, chunk, done):
        sp.dma_start(self.kept[bass.ds(chunk, 1)].rearrange("o c x -> (o c) x"), box[:, :]).then_inc(done, 16)


class ImageStores:
    dmas = IMGS

    def __init__(self, kept):
        self.kept = kept

    def __call__(self, sp, box, chunk, done):
        view = box[:, :].rearrange("p (h n w) -> p h n w", n=IMGS, w=W)
        for n in range(IMGS):
            sp.dma_start(self.kept[bass.ds(chunk * IMGS + n, 1)].rearrange("o c (h w) -> (o c) h w", w=W),
                         view[:, :, n, :]).then_inc(done, 16)


def build(nc, x, w_shift1, w_add1, gamma1, beta1, w_shift2, w_add2, gamma2, beta2, wqkv, b_qkv, b_v, router_w,
          router_b, expert_w, expert_b, out):
    images = x.shape[0]
    chunks = images // IMGS
    kept1 = nc.dram_tensor("kept1", (chunks, C, PIX), F32).ap()
    kept2 = nc.dram_tensor("kept2", (images, C, TOK), F32).ap()

    def image_of(t):
        return lambda n: t[bass.ds(n, 1)].rearrange("o c x -> (o c) x")

    with (
        nc.sbuf_tensor("stats1", [C, chunks * BANKS, 6], F32) as stats1,
        nc.sbuf_tensor("stats2", [C, chunks * BANKS, 6], F32) as stats2,
        nc.sbuf_tensor("bn1", [C, 2], F32) as bn1,
        nc.sbuf_tensor("bn2", [C, 2], F32) as bn2,
    ):
        adder_layer(nc, "l1", chunks, ImageLoads(x), None, w_shift1, w_add1, ChunkStore(kept1), stats1)
        batch_norm_scale(nc, "bn1", stats1, gamma1, beta1, bn1[:, 0:1], bn1[:, 1:2])
        adder_layer(nc, "l2", chunks, ChunkLoad(kept1), (bn1[:, 0:1], bn1[:, 1:2]), w_shift2, w_add2,
                    ImageStores(kept2), stats2)
        batch_norm_scale(nc, "bn2", stats2, gamma2, beta2, bn2[:, 0:1], bn2[:, 1:2])

        token_layer(nc, images, image_of(kept2), image_of(x.rearrange("n c h w -> n c (h w)")), bn2[:, 0:1],
                    bn2[:, 1:2], wqkv, b_qkv, b_v.broadcast_to((TT, C)), router_w, router_b.broadcast_to((TT, E)),
                    expert_w, expert_b, image_of(out.rearrange("n c h w -> n c (h w)")))


def kernel(x, L0_conv_w_shift1, L0_conv_w_add1, L0_conv_bn1_gamma, L0_conv_bn1_beta, L0_conv_w_shift2,
           L0_conv_w_add2, L0_conv_bn2_gamma, L0_conv_bn2_beta, L1_attn_W, L1_attn_b, L1_ffn_router_w,
           L1_ffn_router_b, L1_ffn_expert_w, L1_ffn_expert_b):
    import concourse.bacc as bacc
    from concourse.bass_utils import run_bass_kernel_spmd

    def shift_weights(w):
        return np.asarray(w).transpose(1, 2, 3, 0).reshape(C, TAPS * C)

    def add_weights(w):
        return np.asarray(w).transpose(1, 0, 2, 3).reshape(C, C * TAPS)

    def column(v):
        return np.asarray(v).reshape(C, 1)

    arrays = {
        "x": x,
        "w_shift1": shift_weights(L0_conv_w_shift1), "w_add1": add_weights(L0_conv_w_add1),
        "gamma1": column(L0_conv_bn1_gamma), "beta1": column(L0_conv_bn1_beta),
        "w_shift2": shift_weights(L0_conv_w_shift2), "w_add2": add_weights(L0_conv_w_add2),
        "gamma2": column(L0_conv_bn2_gamma), "beta2": column(L0_conv_bn2_beta),
        "wqkv": np.asarray(L1_attn_W).T, "b_qkv": np.asarray(L1_attn_b).reshape(3, C).T,
        "b_v": np.asarray(L1_attn_b).reshape(3, C)[2:3],
        "router_w": L1_ffn_router_w, "router_b": np.asarray(L1_ffn_router_b).reshape(1, E),
        "expert_w": np.asarray(L1_ffn_expert_w).transpose(1, 0, 2).reshape(C, E * C), "expert_b": L1_ffn_expert_b,
    }
    arrays = {k: np.ascontiguousarray(v) for k, v in arrays.items()}
    nc = bacc.Bacc("TRN2", target_bir_lowering=False, num_devices=1)
    aps = [nc.dram_tensor(k, v.shape, F32, kind="ExternalInput").ap() for k, v in arrays.items()]
    out = nc.dram_tensor("out", arrays["x"].shape, F32, kind="ExternalOutput").ap()
    build(nc, *aps, out)
    return run_bass_kernel_spmd(nc, [arrays], core_ids=[0]).results[0]["out"]
```

```python
import numpy as np
import concourse.bass as bass
from concourse import mybir
from contextlib import ExitStack

F32 = mybir.dt.float32
U32 = mybir.dt.uint32
ALU = mybir.AluOpType
ACT = mybir.ActivationFunctionType
AX = mybir.AxisListType

C = 128
H = W = 28
HP, WP = H + 2, W + 2
TAPS = 9
IMGS = 4
ROWS = H * IMGS
PIX = ROWS * W
PADDED = HP * IMGS * WP
BANKS = 7
BANK_PIX = PIX // BANKS
BANK_ROWS = ROWS // BANKS
BN_EPS = 1e-5
THRESHOLD = 0.005

GROUPS = 4
PER_GROUP = C // GROUPS
JS = 2
STEPS = PER_GROUP // JS
ACT_TAPS = 4
ACT_SLOTS, DVE_SLOTS = 5, 6
TILES = (
    "021000110101300",
    "003011020010110",
    "210100102000021",
    "000212001021001",
)
ACT_AHEAD, DVE_AHEAD = 3, 4
PIECE_ROWS = ROWS // STEPS
PIECE_PIX = PIECE_ROWS * W


def plan():
    taps_done = [0] * GROUPS
    kind_done = [[0, 0] for _ in range(GROUPS)]
    quads, act, dve = [], [], []
    first, last = [len(TILES[0])] * JS, [0] * JS
    for q in range(len(TILES[0])):
        quad = []
        for g in range(GROUPS):
            p = taps_done[g] // TAPS
            k = int(TILES[g][q])
            by_act = k == 0
            start, limit = (0, ACT_TAPS) if by_act else (ACT_TAPS, TAPS)
            n = kind_done[g][by_act]
            taps = tuple(range(start + n, start + n + max(k, 1)))
            assert taps[-1] < limit
            kind_done[g][by_act] += len(taps)
            taps_done[g] += len(taps)
            if taps_done[g] % TAPS == 0:
                kind_done[g] = [0, 0]
            first[p], last[p] = min(first[p], q), max(last[p], q)
            tiles = act if by_act else dve
            quad.append((len(tiles), by_act, p))
            tiles.append((q, p, g, taps))
        quads.append(quad)
    assert taps_done == [JS * TAPS] * GROUPS
    return quads, act, dve, first, last


QUAD_PLAN, ACT_PLAN, DVE_PLAN, FIRST_QUAD, LAST_QUAD = plan()
QUADS = len(QUAD_PLAN)
ACT_TILES, DVE_TILES = len(ACT_PLAN), len(DVE_PLAN)
DVE_SUMS = sum(len(taps) - 1 for _, _, _, taps in DVE_PLAN)


def first_of(tiles, p):
    return min(n for n, tile in enumerate(tiles) if tile[1] == p)


def slot_plan(tiles, slots):
    short = -tiles % slots
    order = []
    runs = [slots] * ((tiles - short * (slots - 1)) // slots) + [slots - 1] * short
    for run in runs:
        order += list(range(run))
    before = []
    for n in range(tiles):
        m = n - 1
        while order[m % tiles] != order[n]:
            m -= 1
        before.append(m)
    return order, before


ACT_SLOT, ACT_BEFORE = slot_plan(ACT_TILES, ACT_SLOTS)
DVE_SLOT, DVE_BEFORE = slot_plan(DVE_TILES, DVE_SLOTS)


def freed_by(before, tiles):
    return tiles[before][0] + 1 if before >= 0 else tiles[before % len(tiles)][0] + 1 - QUADS


def adder_layer(nc, name, chunks, load_chunk, norm, w_shift, w_add, store, stats_out):
    ctx = ExitStack()
    with ctx:
        def sb(n, shape, dt=F32):
            return ctx.enter_context(nc.sbuf_tensor(f"{name}_{n}", shape, dt))

        def sem(n):
            return ctx.enter_context(nc.semaphore(f"{name}_{n}"))

        act_ring = sb("act_ring", [C, ACT_SLOTS, PIX])
        dve_ring = sb("dve_ring", [C, DVE_SLOTS, PIX])
        y = [sb(f"y{i}", [C, HP * IMGS, WP]) for i in range(2)]
        xin = sb("xin", [C, HP * IMGS, WP])
        box = sb("box", [C, PIX])
        wadd = sb("wadd", [C, GROUPS, PER_GROUP, TAPS])
        wq = sb("wq", [C, TAPS, C])
        w_now = sb("w_now", [C, JS, GROUPS, TAPS])
        strip = sb("strip", [C, 2, 2 * PER_GROUP - 1])
        pick = sb("pick", [C, JS, 2, PER_GROUP])
        ones = sb("ones", [C, C])
        zeros = sb("zeros", [1, C])
        wsum_taps = sb("wsum_taps", [C, C])
        wsum = sb("wsum", [C, 1])
        wraw = act_ring[:, 0, 0:TAPS * C]
        wmag = act_ring[:, 1, 0:TAPS * C]
        wpow = act_ring[:, 2, 0:TAPS * C]
        wbit = act_ring[:, 3, 0:TAPS * C]
        wflat = wq[:].rearrange("p t c -> p (t c)")

        psum = ctx.enter_context(nc.psum_tensor(f"{name}_psum", [C, 8, 512], F32))
        dist = psum[:, 0:BANKS, 0:BANK_PIX]
        piece_ps = psum[:, BANKS, 0:PIECE_PIX]

        weights_in = sem("weights_in")
        input_in = sem("input_in")
        normed = sem("normed")
        cleared = sem("cleared")
        wstep = sem("wstep")
        wsum_done = sem("wsum_done")
        piece_done = sem("piece_done")
        piece_kept = sem("piece_kept")
        staged = sem("staged")
        act_tiles = sem("act_tiles")
        dve_tiles = sem("dve_tiles")
        dve_base = sem("dve_base")
        quads_done = sem("quads_done")
        boxed = sem("boxed")
        sums_done = sem("sums_done")
        act_kept = sem("act_kept")
        dve_kept = sem("dve_kept")
        counted = sem("counted")
        stored = sem("stored")
        passed = sem("passed")

        N_ACT_BANKS = (BANKS + 1) // 2
        N_DVE_BANKS = BANKS // 2
        LOADS = load_chunk.dmas
        NORM_STEPS = 2
        BOX_STEPS = TAPS - ACT_TAPS - 1

        def window(buf, tap, row0=0, rows=ROWS):
            dy, dx = tap // 3, tap % 3
            if isinstance(row0, int):
                return buf[:, dy * IMGS + row0:dy * IMGS + row0 + rows, dx:dx + W]
            return buf[:, bass.ds(row0 + dy * IMGS, rows), dx:dx + W]

        def rows_of(flat):
            return flat.rearrange("p (r w) -> p r w", w=W)

        def inner(buf):
            return buf[:, IMGS:IMGS + ROWS, 1:1 + W]

        def over_chunks(eng, body):
            if chunks > 2:
                with eng.Fori(0, chunks // 2 - 1) as i:
                    body(i * 2, 0, True)
                    body(i * 2 + 1, 1, True)
            body(chunks - 2, 0, True)
            body(chunks - 1, 1, False)

        def through_chunks(eng, first, rest, turn, finish):
            first()
            if chunks > 2:
                with eng.Fori(0, chunks // 2 - 1) as i:
                    for parity in range(2):
                        rest(i * 2 + parity, parity, True)
                        turn(i * 2 + parity, parity, True)
            rest(chunks - 2, 0, True)
            turn(chunks - 2, 0, False)
            rest(chunks - 1, 1, False)
            finish(chunks - 1)

        def over_steps(eng, first, last, step):
            with eng.Fori(first, last) as jj:
                step(jj)

        block = ctx.enter_context(nc.Block())

        @block.sync
        def _(sp):
            sp.dma_start(wraw, w_shift).then_inc(weights_in, 16)
            sp.dma_start(wadd[:].rearrange("p g j t -> p (g j t)"), w_add).then_inc(weights_in, 16)
            sp.sem_inc(stored, 16 * store.dmas)
            sp.wait_ge(cleared, 1)
            load_chunk(sp, xin, 0, input_in)
            sp.wait_ge(piece_done, BANKS)
            load_chunk(sp, xin, 1, input_in)

            def chunk_io(c, parity, last_pair):
                if not last_pair:
                    sp.wait_ge(piece_done, BANKS + (c + 1) * STEPS)
                    load_chunk(sp, xin, c + 2, input_in)
                sp.wait_ge(act_kept, (c + 2) * N_ACT_BANKS)
                sp.sem_inc(passed, 1)
                sp.wait_ge(dve_kept, (c + 2) * N_DVE_BANKS)
                store(sp, box, c, stored)

            over_chunks(sp, lambda c, parity, more: chunk_io(c, parity, isinstance(c, int)))
            sp.wait_ge(stored, 16 * store.dmas * (chunks + 1))

        @block.gpsimd
        def _(pool):
            pool.memset(xin[:], 0.0).then_inc(cleared, 1)
            pool.memset(y[0][:], 0.0).then_inc(cleared, 1)
            pool.memset(y[1][:], 0.0).then_inc(cleared, 1)
            pool.memset(ones[:], 1.0).then_inc(cleared, 1)
            pool.memset(zeros[:], 0.0).then_inc(cleared, 1)
            pool.memset(strip[:], 0.0).then_inc(cleared, 1)
            pool.wait_ge(cleared, 6)
            pool.memset(strip[:, 0, PER_GROUP - 1:PER_GROUP], -1.0).then_inc(cleared, 1)
            pool.memset(strip[:, 1, PER_GROUP - 1:PER_GROUP], -2.0).then_inc(cleared, 1)
            pool.wait_ge(cleared, 8)
            pool.wait_ge(weights_in, 32)

            def normalise(c):
                if norm is None:
                    return
                scale, shift = norm
                x = inner(xin)
                pool.wait_ge(input_in, 16 * LOADS * (c + 1))
                pool.sem_inc(passed, 1)
                pool.tensor_scalar(x, x, scale, shift, ALU.mult, ALU.add).then_inc(normed, 1)
                pool.wait_ge(normed, c * NORM_STEPS + 1)
                pool.sem_inc(passed, 1)
                pool.tensor_scalar(x, x, 0.0, None, ALU.max).then_inc(normed, 1)

            def stage(c, jj):
                for p in range(JS):
                    pool.wait_ge(quads_done, (c * STEPS + jj) * QUADS + LAST_QUAD[p] + 1)
                    pool.sem_inc(passed, 1)
                    j = jj * JS + p
                    pool.tensor_copy(w_now[:, p, :, :], wadd[:, :, bass.ds(j, 1), :].rearrange("p g o t -> p g (o t)"))\
                        .then_inc(staged, 1)
                    for s in range(2):
                        pool.tensor_copy(pick[:, p, s, :], strip[:, s, bass.ds(PER_GROUP - 1 - j, PER_GROUP)])\
                            .then_inc(staged, 1)

            def chunk_help(c, parity, more):
                stage(c, 0)
                if more:
                    normalise(c + 1)
                over_steps(pool, 1, STEPS, lambda jj: stage(c, jj))
                pool.wait_ge(piece_kept, BANKS + c * STEPS)
                pool.wait_ge(stored, 16 * store.dmas * (c + 1))
                pool.wait_ge(counted, BANKS * (c + 1))
                src = window(y[parity], ACT_TAPS)
                for n in range(BOX_STEPS):
                    if n:
                        pool.wait_ge(boxed, c * BOX_STEPS + n)
                        src = rows_of(box[:, :])
                    pool.tensor_tensor(rows_of(box[:, :]), src, window(y[parity], ACT_TAPS + 1 + n), ALU.add)\
                        .then_inc(boxed, 1)

            normalise(0)
            over_chunks(pool, chunk_help)

        @block.vector
        def _(dve):
            dve.sem_inc(dve_kept, N_DVE_BANKS)
            dve.sem_inc(counted, BANKS)
            n = [0]

            def link(ins):
                n[0] += 1
                ins.then_inc(wstep, 1)
                dve.wait_ge(wstep, n[0])

            dve.wait_ge(weights_in, 32)
            link(dve.tensor_scalar(wmag.bitcast(U32), wraw.bitcast(U32), 0x7FFFFFFF, None, ALU.bitwise_and))
            link(dve.tensor_scalar(wpow.bitcast(U32), wraw.bitcast(U32), 0x7F800000, None, ALU.bitwise_and))
            link(dve.scalar_tensor_tensor(wbit, wpow, float(np.sqrt(np.float32(2))), wmag, ALU.mult, ALU.is_lt))
            link(dve.scalar_tensor_tensor(wpow, wbit, 1.0, wpow, ALU.add, ALU.mult))
            link(dve.scalar_tensor_tensor(wpow, wmag, THRESHOLD, wpow, ALU.is_ge, ALU.mult))
            link(dve.tensor_scalar(wbit.bitcast(U32), wraw.bitcast(U32), 0x80000000, None, ALU.bitwise_and))
            link(dve.tensor_tensor(wpow.bitcast(U32), wpow.bitcast(U32), wbit.bitcast(U32), ALU.bitwise_or))
            link(dve.tensor_tensor(wpow, wpow, wraw, ALU.subtract))
            link(dve.tensor_tensor(wflat, wraw, wpow, ALU.add))
            link(dve.tensor_reduce(wsum_taps[:, :], wadd[:, :, :, ACT_TAPS:TAPS].rearrange("p g j t -> p (g j) t"),
                                   axis=AX.X, op=ALU.add))
            dve.wait_ge(wsum_done, 1)
            link(dve.tensor_copy(wsum[:, :], psum[:, BANKS, 0:1]))
            dve.wait_ge(cleared, 8)

            for b in range(BANKS):
                dve.wait_ge(piece_done, b + 1)
                dve.tensor_copy(y[0][:, IMGS + b * BANK_ROWS:IMGS + (b + 1) * BANK_ROWS, 1:1 + W], rows_of(dist[:, b, :]))\
                    .then_inc(piece_kept, 1)

            def body(c, parity, more, jj, results_out=None):
                u = c * STEPS + jj
                sums = 0
                for t, (q, p, g, taps) in enumerate(DVE_PLAN):
                    if t == DVE_AHEAD and results_out:
                        results_out()
                    tile = rows_of(dve_ring[:, DVE_SLOT[t], :])
                    if t == first_of(DVE_PLAN, p):
                        dve.wait_ge(staged, u * (3 * JS) + 3 * (p + 1))
                    dve.wait_ge(quads_done, u * QUADS + QUADS + freed_by(DVE_BEFORE[t], DVE_PLAN))
                    tap = taps[0]
                    ins = dve.tensor_scalar(tile, window(y[parity], tap), w_now[:, p, g, tap:tap + 1], None, ALU.max)
                    for tap in taps[1:]:
                        ins.then_inc(dve_base, 1)
                        sums += 1
                        dve.wait_ge(dve_base, u * DVE_SUMS + sums)
                        ins = dve.scalar_tensor_tensor(tile, window(y[parity], tap), w_now[:, p, g, tap:tap + 1], tile,
                                                       ALU.max, ALU.add)
                    ins.then_inc(dve_tiles, 1)
                if more:
                    dve.wait_ge(piece_done, BANKS + u + 1)
                    dve.tensor_copy(y[1 - parity][:, bass.ds(jj * PIECE_ROWS + IMGS, PIECE_ROWS), 1:1 + W],
                                    rows_of(piece_ps)).then_inc(piece_kept, 1)

            def results(c):
                for b in range(1, BANKS, 2):
                    dve.wait_ge(sums_done, c * BANKS + b + 1)
                    dve.tensor_scalar(box[:, b * BANK_PIX:(b + 1) * BANK_PIX], dist[:, b, :], wsum[:, 0:1], None, ALU.add)\
                        .then_inc(dve_kept, 1)

            def statistics(c):
                for b in range(BANKS):
                    if b % 2:
                        dve.wait_ge(dve_kept, (c + 1) * N_DVE_BANKS + b // 2 + 1)
                    else:
                        dve.wait_ge(act_kept, (c + 1) * N_ACT_BANKS + b // 2 + 1)
                    dve.bn_stats(stats_out[:, bass.ds(c * BANKS + b, 1), :].rearrange("p o s -> p (o s)"),
                                 box[:, b * BANK_PIX:(b + 1) * BANK_PIX]).then_inc(counted, 1)

            def y_whole(c):
                dve.wait_ge(piece_kept, BANKS + c * STEPS)
                dve.sem_inc(passed, 1)

            def first():
                y_whole(0)
                body(0, 0, True, 0)

            def rest(c, parity, more):
                over_steps(dve, 1, STEPS, lambda jj: body(c, parity, more, jj))

            def turn(c, parity, more):
                y_whole(c + 1)
                body(c + 1, 1 - parity, more, 0, lambda: results(c))
                statistics(c)

            def finish(c):
                results(c)
                statistics(c)

            through_chunks(dve, first, rest, turn, finish)

        @block.scalar
        def _(act):
            def body(c, parity, jj, results_out=None):
                u = c * STEPS + jj
                for t, (q, p, g, (tap,)) in enumerate(ACT_PLAN):
                    if t == ACT_AHEAD and results_out:
                        results_out()
                    if t == first_of(ACT_PLAN, p):
                        act.wait_ge(staged, u * (3 * JS) + 3 * (p + 1))
                    act.wait_ge(quads_done, u * QUADS + QUADS + freed_by(ACT_BEFORE[t], ACT_PLAN))
                    act.activation(rows_of(act_ring[:, ACT_SLOT[t], :]), window(y[parity], tap), ACT.Abs,
                                   bias=w_now[:, p, g, tap:tap + 1], scale=-1.0).then_inc(act_tiles, 1)

            def results(c):
                for b in range(0, BANKS, 2):
                    act.wait_ge(sums_done, c * BANKS + b + 1)
                    act.activation(box[:, b * BANK_PIX:(b + 1) * BANK_PIX], dist[:, b, :], ACT.Identity,
                                   bias=wsum[:, 0:1], scale=1.0).then_inc(act_kept, 1)

            def y_whole(c):
                act.wait_ge(piece_kept, BANKS + c * STEPS)
                act.sem_inc(passed, 1)

            def first():
                y_whole(0)
                body(0, 0, 0)

            def rest(c, parity, more):
                over_steps(act, 1, STEPS, lambda jj: body(c, parity, jj))

            def turn(c, parity, more):
                y_whole(c + 1)
                body(c + 1, 1 - parity, 0, lambda: results(c))

            act.sem_inc(act_kept, N_ACT_BANKS)
            act.preload_act_table(ACT.Abs)
            act.wait_ge(wstep, 11)
            through_chunks(act, first, rest, turn, results)

        @block.tensor
        def _(pe):
            pe.sem_inc(quads_done, QUADS)
            pe.wait_ge(cleared, 8)
            pe.wait_ge(wstep, 10)
            pe.matmul(psum[:, BANKS, 0:1], wsum_taps[:, :], ones[:, 0:1], start=True, stop=True).then_inc(wsum_done, 1)
            pe.wait_ge(wstep, 11)

            def piece(ps, row0, rows):
                for tap in range(TAPS):
                    last = pe.matmul(rows_of(ps), wq[:, tap, :], window(xin, tap, row0, rows),
                                     start=(tap == 0), stop=(tap == TAPS - 1))
                last.then_inc(piece_done, 1)

            def input_ready(c):
                if norm is None:
                    pe.wait_ge(input_in, 16 * LOADS * (c + 1))
                else:
                    pe.wait_ge(normed, NORM_STEPS * (c + 1))

            input_ready(0)
            for b in range(BANKS):
                piece(dist[:, b, :], b * BANK_ROWS, BANK_ROWS)

            def next_piece(c, jj):
                input_ready(c + 1)
                pe.wait_ge(piece_kept, BANKS + c * STEPS + jj)
                piece(piece_ps, jj * PIECE_ROWS, PIECE_ROWS)

            def quads(c, jj):
                u = c * STEPS + jj
                for q, quad in enumerate(QUAD_PLAN):
                    for p in range(JS):
                        if q == FIRST_QUAD[p]:
                            pe.wait_ge(staged, u * (3 * JS) + 3 * (p + 1))
                    pe.wait_ge(act_tiles, u * ACT_TILES + sum(t[0] <= q for t in ACT_PLAN))
                    pe.wait_ge(dve_tiles, u * DVE_TILES + sum(t[0] <= q for t in DVE_PLAN))
                    for b in range(BANKS):
                        for g, (t, is_act, p) in enumerate(quad):
                            tile = act_ring[:, ACT_SLOT[t], :] if is_act else dve_ring[:, DVE_SLOT[t], :]
                            last = pe.matmul(dist[PER_GROUP * g:PER_GROUP * (g + 1), b, :],
                                             pick[:, p, 0 if is_act else 1, :],
                                             tile[:, b * BANK_PIX:(b + 1) * BANK_PIX], start=False, stop=False,
                                             skip_group_check=True)
                    last.then_inc(quads_done, 1)

            def open_sums(c):
                for b in range(BANKS):
                    if b % 2:
                        pe.wait_ge(dve_kept, c * N_DVE_BANKS + b // 2 + 1)
                    else:
                        pe.wait_ge(act_kept, c * N_ACT_BANKS + b // 2 + 1)
                    pe.matmul(dist[:, b, 0:1], zeros[:, :], ones[0:1, 0:1], start=True, stop=False,
                              skip_group_check=True)

            def first():
                next_piece(0, 0)
                pe.wait_ge(piece_kept, BANKS)
                open_sums(0)
                quads(0, 0)

            def step(c, more, jj):
                if more:
                    next_piece(c, jj)
                quads(c, jj)

            def rest(c, parity, more):
                over_steps(pe, 1, STEPS, lambda jj: step(c, more, jj))

            def close_sums(c):
                pe.wait_ge(boxed, c * BOX_STEPS + BOX_STEPS)
                for b in range(BANKS):
                    pe.matmul(dist[:, b, :], ones[:, :], box[:, b * BANK_PIX:(b + 1) * BANK_PIX], start=False,
                              stop=True, skip_group_check=True).then_inc(sums_done, 1)

            def turn(c, parity, more):
                close_sums(c)
                if more:
                    next_piece(c + 1, 0)
                open_sums(c + 1)
                quads(c + 1, 0)

            through_chunks(pe, first, rest, turn, close_sums)


TOK = H * W
TT = 112
NT = TOK // TT
PER_BANK = 4
SPLIT = PER_BANK * TT
E = 8
ACT_E = PER_BANK
DVE_E = E - ACT_E
LATE = 5
V1 = C + 1
O_BANK = 3
LN_EPS = 1e-5
DEN_EPS = 1e-6


def batch_norm_scale(nc, name, stats, gamma, beta, scale, shift):
    with (
        nc.sbuf_tensor(f"{name}_mv", [C, 2], F32) as mv,
        nc.sbuf_tensor(f"{name}_gb", [C, 2], F32) as gb,
        nc.sbuf_tensor(f"{name}_half", [C, 1], F32) as half,
        nc.sbuf_tensor(f"{name}_rstd", [C, 1], F32) as rstd,
        nc.semaphore(f"{name}_params_in") as params_in,
        nc.semaphore(f"{name}_mv_ready") as mv_ready,
        nc.semaphore(f"{name}_half_ready") as half_ready,
        nc.semaphore(f"{name}_rstd_ready") as rstd_ready,
        nc.semaphore(f"{name}_scaled") as scaled,
        nc.Block() as block,
    ):
        @block.sync
        def _(sp):
            sp.dma_start(gb[:, 0:1], gamma).then_inc(params_in, 16)
            sp.dma_start(gb[:, 1:2], beta).then_inc(params_in, 16)

        @block.gpsimd
        def _(pool):
            pool.memset(half[:], -0.5).then_inc(half_ready, 1)
            pool.wait_ge(half_ready, 1)
            pool.wait_ge(mv_ready, 2)
            pool.tensor_tensor(rstd[:], mv[:, 1:2], half[:], ALU.pow).then_inc(rstd_ready, 1)

        @block.vector
        def _(dve):
            dve.bn_aggr(mv[:], stats[:].rearrange("p n s -> p (n s)")).then_inc(mv_ready, 1)
            dve.wait_ge(mv_ready, 1)
            dve.tensor_scalar(mv[:, 1:2], mv[:, 1:2], BN_EPS, None, ALU.add).then_inc(mv_ready, 1)
            dve.wait_ge(rstd_ready, 1)
            dve.wait_ge(params_in, 32)
            dve.tensor_tensor(scale, gb[:, 0:1], rstd[:], ALU.mult).then_inc(scaled, 1)
            dve.wait_ge(scaled, 1)
            dve.tensor_tensor(shift, mv[:, 0:1], scale, ALU.mult).then_inc(scaled, 1)
            dve.wait_ge(scaled, 2)
            dve.tensor_tensor(shift, gb[:, 1:2], shift, ALU.subtract).then_inc(scaled, 1)


def token_layer(nc, images, conv_image, x_image, scale, shift, wqkv, b_qkv, b_v, router_w, router_b,
                expert_w, expert_b, out_image):
    ctx = ExitStack()
    with ctx:
        def sb(n, shape, dt=F32):
            return ctx.enter_context(nc.sbuf_tensor(f"t_{n}", shape, dt))

        def sem(n):
            return ctx.enter_context(nc.semaphore(f"t_{n}"))

        ident = sb("ident", [C, C])
        causal = sb("causal", [TT, TT])
        minus_half = sb("minus_half", [TT, NT])
        rank = sb("rank", [TT, E])
        w_qkv = sb("w_qkv", [C, 3, C])
        bias_qk = sb("bias_qk", [C, 3])
        bias_qk1 = sb("bias_qk1", [C, 3])
        minus_bias = sb("minus_bias", [C, 3])
        bias_v = sb("bias_v", [TT, C])
        w_router = sb("w_router", [C, E])
        bias_router = sb("bias_router", [TT, E])
        w_expert = sb("w_expert", [C, E * C])
        bias_expert = sb("bias_expert", [NT * E, NT * C])

        conv_in = sb("conv_in", [C, TOK])
        x_in = sb("x_in", [C, TOK])
        pre = sb("pre", [C, TOK])
        t_ch = sb("t_ch", [C, TOK])
        t_tok = sb("t_tok", [TT, NT, C])
        st_a = sb("st_a", [TT, NT, 6])
        mv_a = sb("mv_a", [TT, NT, 2])
        var_a = sb("var_a", [TT, NT])
        rstd_a = sb("rstd_a", [TT, NT])
        norm_a = sb("norm_a", [TT, NT, C])
        norm_a_ch = sb("norm_a_ch", [C, TOK])
        low = [sb(f"low_{s}", [C, TOK]) for s in "qk"]
        qk = [sb(f"{s}_ch", [C, TOK]) for s in "qk"]
        q_ch, k_ch = qk
        k_tok = sb("k_tok", [TT, NT, C])
        v_tok = sb("v_tok", [TT, NT, V1])
        score = sb("score", [TT, NT, TT])
        state = sb("state", [C, NT, V1])
        den = sb("den", [TT, 9])
        rden = sb("rden", [TT, NT])
        t2 = sb("t2", [TT, NT, C])

        st_b = sb("st_b", [TT, NT, 6])
        mv_b = sb("mv_b", [TT, NT, 2])
        var_b = sb("var_b", [TT, NT])
        rstd_b = sb("rstd_b", [TT, NT])
        norm_b = sb("norm_b", [TT, NT, C])
        norm_b_ch = sb("norm_b_ch", [C, TOK])
        prob = sb("prob", [TT, NT, E])
        work = sb("work", [TT, NT, E])
        mask1 = sb("mask1", [TT, NT, E])
        mask2 = sb("mask2", [TT, NT, E])
        top = sb("top", [TT, 4, NT])
        gate = sb("gate", [TT, NT, E])
        gate_t = sb("gate_t", [NT * E, TT])
        scaled = sb("scaled", [TT, NT, ACT_E, C])
        t3 = sb("t3", [TT, NT, C])
        out_ch = sb("out_ch", [C, TOK])

        psum = ctx.enter_context(nc.psum_tensor("t_psum", [C, 8, 512], F32))

        def by_channels(bank):
            return [(slice(0, SPLIT), psum[:, bank, 0:SPLIT]), (slice(SPLIT, TOK), psum[:, bank + 1, 0:TOK - SPLIT])]

        def ch_tile(bank, t):
            return psum[:, bank + t // PER_BANK, (t % PER_BANK) * TT:(t % PER_BANK + 1) * TT]

        def by_tokens(bank):
            return psum[0:TT, bank:bank + 2, :].rearrange("p b (t c) -> p (b t) c", c=C)[:, 0:NT, :]

        def tok_tile(bank, t):
            return psum[0:TT, bank + t // PER_BANK, (t % PER_BANK) * C:(t % PER_BANK + 1) * C]

        def score_tile(t):
            return psum[0:TT, t // PER_BANK, (t % PER_BANK) * TT:(t % PER_BANK + 1) * TT]

        def state_tile(t):
            return psum[:, 2 + t // O_BANK, (t % O_BANK) * V1:(t % O_BANK + 1) * V1]

        def o_tile(t):
            return psum[0:TT, t // O_BANK, (t % O_BANK) * V1:(t % O_BANK + 1) * V1]

        def cols(t):
            return slice(t * TT, (t + 1) * TT)

        T01, B23, EXPERTS, B67 = 0, 2, 4, 6
        logits_ps = psum[0:TT, B67, 0:NT * E].rearrange("p (t e) -> p t e", e=E)
        gate_ps = psum[0:NT * E, B67 + 1, 0:TT]

        consts_in = sem("consts_in")
        const_made = sem("const_made")
        const_sum = sem("const_sum")
        loaded = sem("loaded")
        pre_ready = sem("pre_ready")
        t_ch_ready = sem("t_ch_ready")
        t_ps = sem("t_ps")
        t_tok_ready = sem("t_tok_ready")
        stat_a = sem("stat_a")
        var_a_made = sem("var_a_made")
        rstd_a_ready = sem("rstd_a_ready")
        norm_a_ready = sem("norm_a_ready")
        norm_a_ps = sem("norm_a_ps")
        norm_a_ch_ready = sem("norm_a_ch_ready")
        qk_ps = sem("qk_ps")
        low_ready = sem("low_ready")
        exp_ready = sem("exp_ready")
        qk_ready = sem("qk_ready")
        v_ps = sem("v_ps")
        v_ready = sem("v_ready")
        k_ps = sem("k_ps")
        k_tok_ready = sem("k_tok_ready")
        score_ps = sem("score_ps")
        score_ready = sem("score_ready")
        state_ps = sem("state_ps")
        state_step = sem("state_step")
        o_ps = sem("o_ps")
        den_step = sem("den_step")
        t2_ready = sem("t2_ready")
        stat_b = sem("stat_b")
        var_b_made = sem("var_b_made")
        rstd_b_ready = sem("rstd_b_ready")
        norm_b_ready = sem("norm_b_ready")
        norm_b_ps = sem("norm_b_ps")
        norm_b_ch_ready = sem("norm_b_ch_ready")
        logits_made = sem("logits_made")
        gate_step = sem("gate_step")
        prob_exp = sem("prob_exp")
        gate_t_made = sem("gate_t_made")
        gate_t_ready = sem("gate_t_ready")
        expert_made = sem("expert_made")
        t2_kept = sem("t2_kept")
        acc_step = sem("acc_step")
        scaled_ready = sem("scaled_ready")
        out_ps = sem("out_ps")
        out_ch_ready = sem("out_ch_ready")
        out_stored = sem("out_stored")
        passed = sem("passed")
        GATE_STEPS = 24
        ACC_STEPS = NT * DVE_E

        def pipelined(eng, pre, phase1, phase2):
            pre(0)
            phase1(0, None, None)
            phase2(0, None, 1)
            phase1(1, 0, None)
            with eng.Fori(0, images - 2) as i:
                phase2(i + 1, i, i + 2)
                phase1(i + 2, i + 1, i)
            phase2(images - 1, images - 2, None)
            phase1(None, images - 1, images - 2)
            phase2(None, images - 1, None)
            phase1(None, None, images - 1)

        block = ctx.enter_context(nc.Block())

        @block.sync
        def _(sp):
            def load(n):
                sp.dma_start(conv_in[:, :], conv_image(n)).then_inc(loaded, 16)
                sp.dma_start(x_in[:, :], x_image(n)).then_inc(loaded, 16)

            def keep(n):
                sp.wait_ge(out_ch_ready, n + 2)
                sp.dma_start(out_image(n), out_ch[:, :]).then_inc(out_stored, 16)

            sp.sem_inc(out_stored, 16)
            load(0)
            sp.dma_start(w_qkv[:].rearrange("p s c -> p (s c)"), wqkv).then_inc(consts_in, 16)
            sp.dma_start(bias_qk[:, :], b_qkv).then_inc(consts_in, 16)
            sp.dma_start(bias_v[:, :], b_v).then_inc(consts_in, 16)
            sp.dma_start(w_router[:, :], router_w).then_inc(consts_in, 16)
            sp.dma_start(bias_router[:, :], router_b).then_inc(consts_in, 16)
            sp.dma_start(w_expert[:, :], expert_w).then_inc(consts_in, 16)
            sp.wait_ge(const_made, 8)
            for t in range(NT):
                sp.dma_start(bias_expert[t * E:(t + 1) * E, t * C:(t + 1) * C], expert_b).then_inc(consts_in, 16)
            sp.wait_ge(pre_ready, 1)
            load(1)
            with sp.Fori(0, images - 2) as i:
                sp.wait_ge(pre_ready, i + 2)
                load(i + 2)
                keep(i)
            keep(images - 2)
            keep(images - 1)
            sp.wait_ge(out_stored, 16 * (images + 1))

        CONSTS = 16 * (6 + NT)

        @block.gpsimd
        def _(pool):
            pool.memset(ident[:], 0.0).then_inc(const_made, 1)
            pool.memset(causal[:], 1.0).then_inc(const_made, 1)
            pool.memset(minus_half[:], -0.5).then_inc(const_made, 1)
            pool.memset(bias_expert[:], 0.0).then_inc(const_made, 1)
            pool.memset(v_tok[:, :, C:V1], 1.0).then_inc(const_made, 1)
            pool.memset(rank[:], 1.0).then_inc(const_made, 1)
            pool.wait_ge(const_made, 6)
            pool.affine_select(out=ident[:], in_=ident[:], compare_op=ALU.not_equal, fill=1.0, base=0,
                               pattern=[[-1, C]], channel_multiplier=1).then_inc(const_made, 1)
            pool.affine_select(out=causal[:], in_=causal[:], compare_op=ALU.is_ge, fill=0.0, base=0,
                               pattern=[[1, TT]], channel_multiplier=-1).then_inc(const_made, 1)
            for e in range(E - 1):
                pool.memset(rank[:, e:e + 1], float(E - e)).then_inc(const_made, 1)

            def rstd(n, stat, mv, var, var_made, out, ready):
                pool.wait_ge(stat, 2 * NT * (n + 1))
                pool.sem_inc(passed, 1)
                pool.tensor_scalar(var[:], mv[:, :, 1], LN_EPS, None, ALU.add).then_inc(var_made, 1)
                pool.wait_ge(var_made, n + 1)
                pool.tensor_tensor(out[:], var[:], minus_half[:], ALU.pow).then_inc(ready, 1)

            def rstd_of_a(n):
                rstd(n, stat_a, mv_a, var_a, var_a_made, rstd_a, rstd_a_ready)

            def rstd_of_b(n):
                rstd(n, stat_b, mv_b, var_b, var_b_made, rstd_b, rstd_b_ready)

            def pre(n):
                pass

            def phase1(c, a, b):
                if a is not None:
                    rstd_of_b(a)
                if c is not None:
                    rstd_of_a(c)

            def phase2(a, b, c):
                pass

            pipelined(pool, pre, phase1, phase2)

        @block.vector
        def _(dve):
            def a_pre(n):
                dve.wait_ge(loaded, 32 * (n + 1))
                dve.scalar_tensor_tensor(pre[:, :], conv_in[:, :], scale, x_in[:, :], ALU.mult, ALU.add)\
                    .then_inc(pre_ready, 1)

            def stats(n, src, st, mv, stat):
                for t in range(NT):
                    dve.bn_stats(st[:, t, :], src[:, t, :]).then_inc(stat, 1)
                for t in range(NT):
                    if t == 0:
                        dve.wait_ge(stat, 2 * NT * n + NT)
                        dve.sem_inc(passed, 1)
                    dve.bn_aggr(mv[:, t, :], st[:, t, :]).then_inc(stat, 1)

            def normalise(src, mv, rstd, out, ready):
                for t in range(NT):
                    last = dve.tensor_scalar(out[:, t, :], src[:, t, :], mv[:, t, 0:1], rstd[:, t:t + 1],
                                             ALU.subtract, ALU.mult)
                last.then_inc(ready, 1)

            def a_stats(n):
                dve.wait_ge(t_tok_ready, n + 1)
                stats(n, t_tok, st_a, mv_a, stat_a)

            def a_norm(n):
                dve.wait_ge(rstd_a_ready, n + 1)
                normalise(t_tok, mv_a, rstd_a, norm_a, norm_a_ready)

            def a_elu(n):
                for s, bank in ((0, T01), (1, B23)):
                    dve.wait_ge(exp_ready, 2 * n + s + 1)
                    for at, ps in by_channels(bank):
                        last = dve.scalar_tensor_tensor(qk[s][:, at], ps, bias_qk1[:, s:s + 1], low[s][:, at],
                                                        ALU.add, ALU.max)
                    last.then_inc(qk_ready, 1)

            def a_v(n):
                dve.wait_ge(v_ps, n + 1)
                dve.tensor_tensor(v_tok[:, :, 0:C], by_tokens(EXPERTS),
                                  bias_v[:, :].rearrange("p (o c) -> p o c", o=1).broadcast_to((TT, NT, C)), ALU.add)\
                    .then_inc(v_ready, 1)

            def a_scores(n):
                dve.wait_ge(score_ps, n + 1)
                mask = causal[:, :].rearrange("p (o c) -> p o c", o=1)
                for t, k in ((0, PER_BANK), (PER_BANK, NT - PER_BANK)):
                    last = dve.tensor_tensor(score[:, t:t + k, :],
                                             psum[0:TT, t // PER_BANK, 0:k * TT].rearrange("p (t c) -> p t c", c=TT),
                                             mask.broadcast_to((TT, k, TT)), ALU.mult)
                last.then_inc(score_ready, 1)

            def a_state(n):
                dve.wait_ge(state_ps, n + 1)
                dve.tensor_copy(state[:, 1, :], state_tile(0)).then_inc(state_step, 1)
                for t in range(2, NT):
                    dve.wait_ge(state_step, (NT - 1) * n + t - 1)
                    dve.tensor_tensor(state[:, t, :], state_tile(t - 1), state[:, t - 1, :], ALU.add)\
                        .then_inc(state_step, 1)

            def a_out(n):
                dve.wait_ge(o_ps, n + 1)
                full = psum[0:TT, 0:2, 0:O_BANK * V1].rearrange("p b (t c) -> p b t c", c=V1)[:, :, :, C:V1]
                dve.tensor_scalar(den[:, 0:6].rearrange("p (b t o) -> p b t o", b=2, o=1), full, DEN_EPS, None, ALU.add)\
                    .then_inc(den_step, 1)
                dve.tensor_scalar(den[:, 6:7], o_tile(6)[:, C:V1], DEN_EPS, None, ALU.add).then_inc(den_step, 1)
                dve.wait_ge(den_step, 3 * n + 2)
                dve.reciprocal(rden[:, :], den[:, 0:NT]).then_inc(den_step, 1)
                dve.wait_ge(den_step, 3 * n + 3)
                for t in range(NT):
                    last = dve.scalar_tensor_tensor(t2[:, t, :], o_tile(t)[:, 0:C], rden[:, t:t + 1], t_tok[:, t, :],
                                                    ALU.mult, ALU.add)
                last.then_inc(t2_ready, 1)

            def b_stats(n):
                dve.wait_ge(t2_ready, n + 1)
                stats(n, t2, st_b, mv_b, stat_b)

            def b_norm(n):
                dve.wait_ge(rstd_b_ready, n + 1)
                normalise(t2, mv_b, rstd_b, norm_b, norm_b_ready)

            def b_router(n):
                at = [0]

                def step(ins):
                    at[0] += 1
                    ins.then_inc(gate_step, 1)
                    dve.wait_ge(gate_step, GATE_STEPS * n + at[0])

                def per_expert(x):
                    return x.rearrange("p (t o) -> p t o", o=1).broadcast_to((TT, NT, E))

                ranks = rank[:, :].rearrange("p (o e) -> p o e", o=1).broadcast_to((TT, NT, E))
                biases = bias_router[:, :].rearrange("p (o e) -> p o e", o=1).broadcast_to((TT, NT, E))
                some, first, second, total = (top[:, i, :] for i in range(4))

                def highest(out, x):
                    step(dve.tensor_reduce(out, x[:, :, :], axis=AX.X, op=ALU.max))

                dve.wait_ge(logits_made, n + 1)
                step(dve.tensor_tensor(prob[:, :, :], logits_ps, biases, ALU.add))
                highest(some, prob)
                step(dve.tensor_tensor(prob[:, :, :], prob[:, :, :], per_expert(some), ALU.subtract))
                dve.wait_ge(prob_exp, n + 1)
                step(dve.tensor_reduce(total, prob[:, :, :], axis=AX.X, op=ALU.add))
                step(dve.reciprocal(total, total))
                step(dve.tensor_tensor(prob[:, :, :], prob[:, :, :], per_expert(total), ALU.mult))
                for value, mask in ((first, mask1), (second, mask2)):
                    highest(value, prob)
                    step(dve.tensor_tensor(work[:, :, :], prob[:, :, :], per_expert(value), ALU.is_equal))
                    step(dve.tensor_tensor(work[:, :, :], work[:, :, :], ranks, ALU.mult))
                    highest(some, work)
                    step(dve.tensor_tensor(mask[:, :, :], work[:, :, :], per_expert(some), ALU.is_equal))
                    if mask is mask1:
                        step(dve.scalar_tensor_tensor(prob[:, :, :], mask[:, :, :], -2.0, prob[:, :, :], ALU.mult, ALU.add))
                step(dve.tensor_tensor(total, first, second, ALU.add))
                step(dve.reciprocal(total, total))
                step(dve.tensor_tensor(first, first, total, ALU.mult))
                step(dve.tensor_tensor(second, second, total, ALU.mult))
                step(dve.tensor_tensor(gate[:, :, :], mask1[:, :, :], per_expert(first), ALU.mult))
                step(dve.tensor_tensor(work[:, :, :], mask2[:, :, :], per_expert(second), ALU.mult))
                step(dve.tensor_tensor(gate[:, :, :], gate[:, :, :], work[:, :, :], ALU.add))
                assert at[0] == GATE_STEPS

            def b_keep(n):
                dve.tensor_copy(t3[:, LATE:NT, :], t2[:, LATE:NT, :]).then_inc(t2_kept, 1)

            def b_tile(n, t):
                for e in range(ACT_E, E):
                    if e == ACT_E:
                        dve.wait_ge(expert_made, 2 * NT * n + 2 * t + 2)
                    if e > ACT_E:
                        dve.wait_ge(acc_step, ACC_STEPS * n + DVE_E * (t + 1) + e - ACT_E)
                    if e == ACT_E and t >= LATE:
                        dve.wait_ge(t2_kept, n + 1)
                    src = t3 if e > ACT_E or t >= LATE else t2
                    dve.scalar_tensor_tensor(
                        t3[:, t, :], psum[0:TT, EXPERTS + 1, (e - ACT_E) * C:(e - ACT_E + 1) * C],
                        gate[:, t, e:e + 1], src[:, t, :], ALU.mult, ALU.add).then_inc(acc_step, 1)

            def phase1(c, a, b):
                if a is not None:
                    b_stats(a)
                if b is not None:
                    b_tile(b, LATE)
                if c is not None:
                    a_stats(c)
                if b is not None:
                    for t in range(LATE + 1, NT):
                        b_tile(b, t)
                if a is not None:
                    b_norm(a)
                if c is not None:
                    a_norm(c)
                if a is not None:
                    b_router(a)
                if c is not None:
                    a_v(c)
                    a_elu(c)

            def phase2(a, b, c):
                if b is not None:
                    b_tile(b, 0)
                if a is not None:
                    a_scores(a)
                if b is not None:
                    b_tile(b, 1)
                if a is not None:
                    a_state(a)
                if b is not None:
                    for t in range(2, 4):
                        b_tile(b, t)
                if c is not None:
                    a_pre(c)
                if b is not None:
                    for t in range(4, LATE):
                        b_tile(b, t)
                    b_keep(b)
                if a is not None:
                    a_out(a)

            dve.sem_inc(acc_step, DVE_E)
            dve.wait_ge(consts_in, CONSTS)
            dve.wait_ge(const_made, 8 + E - 1)
            dve.tensor_scalar(bias_qk1[:, :], bias_qk[:, :], 1.0, None, ALU.add).then_inc(const_sum, 1)
            dve.tensor_scalar(minus_bias[:, :], bias_qk[:, :], -1.0, None, ALU.mult).then_inc(const_sum, 1)
            dve.wait_ge(const_sum, 2)
            pipelined(dve, a_pre, phase1, phase2)

        @block.scalar
        def _(act):
            def a_relu(n):
                act.wait_ge(pre_ready, n + 1)
                act.activation(t_ch[:, :], pre[:, :], ACT.Relu, bias=shift, scale=1.0).then_inc(t_ch_ready, 1)

            def a_t_tok(n):
                act.wait_ge(t_ps, n + 1)
                act.copy(t_tok[:, :, :], by_tokens(T01)).then_inc(t_tok_ready, 1)

            def keep_channels(out, bank, made, at_least, ready):
                act.wait_ge(made, at_least)
                for at, ps in by_channels(bank):
                    last = act.copy(out[:, at], ps)
                last.then_inc(ready, 1)

            def a_norm(n):
                keep_channels(norm_a_ch, B23, norm_a_ps, n + 1, norm_a_ch_ready)

            def a_exp(n):
                for s, bank in ((0, T01), (1, B23)):
                    act.wait_ge(qk_ps, 2 * n + s + 1)
                    for at, ps in by_channels(bank):
                        last = act.activation(low[s][:, at], ps, ACT.Relu, bias=minus_bias[:, s:s + 1], scale=-1.0)
                    last.then_inc(low_ready, 1)
                for s in range(2):
                    act.wait_ge(low_ready, 2 * n + s + 1)
                    act.activation(low[s][:, :], low[s][:, :], ACT.Exp, scale=-1.0).then_inc(exp_ready, 1)

            def a_k(n):
                act.wait_ge(k_ps, n + 1)
                act.copy(k_tok[:, :, :], by_tokens(B23)).then_inc(k_tok_ready, 1)

            def b_norm(n):
                keep_channels(norm_b_ch, T01, norm_b_ps, n + 1, norm_b_ch_ready)

            def b_prob(n):
                act.wait_ge(gate_step, GATE_STEPS * n + 3)
                act.activation(prob[:, :, :], prob[:, :, :], ACT.Exp).then_inc(prob_exp, 1)

            def b_gate(n):
                act.wait_ge(gate_t_made, n + 1)
                act.copy(gate_t[:, :], gate_ps).then_inc(gate_t_ready, 1)

            def b_tile(n, t):
                act.wait_ge(expert_made, 2 * NT * n + 2 * t + 1)
                for e in range(ACT_E):
                    last = act.activation(scaled[:, t, e, :], psum[0:TT, EXPERTS, e * C:(e + 1) * C], ACT.Identity, bias=0.0,
                                          scale=gate[:, t, e:e + 1])
                last.then_inc(scaled_ready, 1)

            def b_out(n):
                act.wait_ge(out_stored, 16 * (n + 1))
                keep_channels(out_ch, B67, out_ps, n + 1, out_ch_ready)

            def phase1(c, a, b):
                if c is not None:
                    a_t_tok(c)
                if b is not None:
                    for t in range(LATE, NT):
                        b_tile(b, t)
                    b_out(b)
                if a is not None:
                    b_norm(a)
                if c is not None:
                    a_norm(c)
                if a is not None:
                    b_prob(a)
                if c is not None:
                    a_exp(c)
                if a is not None:
                    b_gate(a)

            def phase2(a, b, c):
                if b is not None:
                    b_tile(b, 0)
                if a is not None:
                    a_k(a)
                if b is not None:
                    for t in range(1, 4):
                        b_tile(b, t)
                if c is not None:
                    a_relu(c)
                if b is not None:
                    for t in range(4, LATE):
                        b_tile(b, t)

            act.sem_inc(out_ch_ready, 1)
            act.sem_inc(scaled_ready, 1)
            act.wait_ge(const_sum, 2)
            act.preload_act_table(ACT.Exp)
            pipelined(act, a_relu, phase1, phase2)

        @block.tensor
        def _(pe):
            def to_channels(src, bank, ready, at_least, made):
                pe.wait_ge(ready, at_least)
                for t in range(NT):
                    last = pe.transpose(ch_tile(bank, t), src[:, t, :], ident[0:TT, 0:TT])
                last.then_inc(made, 1)

            def to_tokens(src, bank, made):
                for t in range(NT):
                    last = pe.transpose(tok_tile(bank, t), src[:, cols(t)], ident[:, :])
                last.then_inc(made, 1)

            def a_t(n):
                pe.wait_ge(t_ch_ready, n + 1)
                if not isinstance(n, int) or n > 0:
                    pe.wait_ge(t2_ready, n)
                to_tokens(t_ch, T01, t_ps)

            def a_norm(n):
                to_channels(norm_a, B23, norm_a_ready, n + 1, norm_a_ps)

            def a_qk(n):
                pe.wait_ge(norm_a_ch_ready, n + 1)
                for s, bank in ((0, T01), (1, B23)):
                    for at, ps in by_channels(bank):
                        last = pe.matmul(ps, w_qkv[:, s, :], norm_a_ch[:, at], start=True, stop=True)
                    last.then_inc(qk_ps, 1)

            def a_v(n):
                for t in range(NT):
                    last = pe.matmul(tok_tile(EXPERTS, t), norm_a_ch[:, cols(t)], w_qkv[:, 2, :], start=True, stop=True)
                last.then_inc(v_ps, 1)

            def a_k(n):
                pe.wait_ge(qk_ready, 2 * n + 2)
                to_tokens(k_ch, B23, k_ps)

            def a_scores(n):
                for t in range(NT):
                    last = pe.matmul(score_tile(t), k_ch[:, cols(t)], q_ch[:, cols(t)], start=True, stop=True)
                last.then_inc(score_ps, 1)

            def a_state(n):
                pe.wait_ge(k_tok_ready, n + 1)
                pe.wait_ge(v_ready, n + 1)
                for t in range(NT - 1):
                    last = pe.matmul(state_tile(t), k_tok[:, t, :], v_tok[:, t, :], start=True, stop=True)
                last.then_inc(state_ps, 1)

            def a_out(n):
                pe.wait_ge(score_ready, n + 1)
                pe.wait_ge(state_step, (NT - 1) * (n + 1))
                for t in range(NT):
                    last = pe.matmul(o_tile(t), score[:, t, :], v_tok[:, t, :], start=True, stop=(t == 0))
                    if t:
                        last = pe.matmul(o_tile(t), q_ch[:, cols(t)], state[:, t, :], start=False, stop=True)
                last.then_inc(o_ps, 1)

            def b_norm(n):
                to_channels(norm_b, T01, norm_b_ready, n + 1, norm_b_ps)

            def b_router(n):
                pe.wait_ge(out_ch_ready, n + 1)
                pe.wait_ge(norm_b_ch_ready, n + 1)
                for t in range(NT):
                    last = pe.matmul(logits_ps[:, t, :], norm_b_ch[:, cols(t)], w_router[:, :], start=True, stop=True)
                last.then_inc(logits_made, 1)

            def b_gates(n):
                pe.wait_ge(gate_step, GATE_STEPS * (n + 1))
                pe.sem_inc(passed, 1)
                pe.transpose(gate_ps, gate[:, :, :].rearrange("p t e -> p (t e)"), ident[0:TT, 0:TT])\
                    .then_inc(gate_t_made, 1)

            def b_experts(n, t):
                for half in range(2):
                    if half == 0:
                        pe.wait_ge(scaled_ready, NT * n + t + 1)
                    else:
                        pe.wait_ge(acc_step, ACC_STEPS * n + DVE_E * (t + 1))
                    pe.matmul(psum[0:TT, EXPERTS + half, :], norm_b_ch[:, cols(t)],
                              w_expert[:, half * PER_BANK * C:(half + 1) * PER_BANK * C], start=True, stop=True)\
                        .then_inc(expert_made, 1)

            def b_sum(n, t):
                if t == 0:
                    pe.wait_ge(gate_t_ready, n + 1)
                pe.matmul(ch_tile(B67, t), bias_expert[:, t * C:(t + 1) * C], gate_t[:, :], start=True, stop=False)
                pe.wait_ge(scaled_ready, NT * n + t + 2)
                for e in range(ACT_E):
                    pe.matmul(ch_tile(B67, t), scaled[:, t, e, :], ident[0:TT, 0:TT], start=False, stop=False)
                pe.wait_ge(acc_step, ACC_STEPS * n + DVE_E * (t + 2))
                last = pe.matmul(ch_tile(B67, t), t3[:, t, :], ident[0:TT, 0:TT], start=False, stop=True)
                if t == NT - 1:
                    last.then_inc(out_ps, 1)

            def pre(n):
                pass

            def phase1(c, a, b):
                if b is not None:
                    b_experts(b, LATE)
                    b_sum(b, LATE - 1)
                if c is not None:
                    a_t(c)
                if b is not None:
                    for t in range(LATE + 1, NT):
                        b_experts(b, t)
                        b_sum(b, t - 1)
                    b_sum(b, NT - 1)
                if a is not None:
                    b_norm(a)
                if c is not None:
                    a_norm(c)
                if a is not None:
                    b_router(a)
                if c is not None:
                    a_qk(c)
                    a_v(c)
                if a is not None:
                    b_gates(a)

            def phase2(a, b, c):
                if a is not None:
                    pe.wait_ge(v_ready, a + 1)
                if b is not None:
                    b_experts(b, 0)
                if a is not None:
                    a_k(a)
                    a_scores(a)
                if b is not None:
                    b_experts(b, 1)
                if a is not None:
                    a_state(a)
                if b is not None:
                    for t in range(1, 3):
                        b_sum(b, t - 1)
                        b_experts(b, t + 1)
                if a is not None:
                    a_out(a)
                if b is not None:
                    b_sum(b, 2)
                    for t in range(4, LATE):
                        b_experts(b, t)
                        b_sum(b, t - 1)

            pe.wait_ge(consts_in, CONSTS)
            pe.wait_ge(const_made, 8 + E - 1)
            pipelined(pe, pre, phase1, phase2)


class ImageLoads:
    dmas = IMGS

    def __init__(self, x):
        self.x = x

    def __call__(self, sp, xin, chunk, done):
        view = xin[:].rearrange("p (h n) w -> p h n w", n=IMGS)
        for n in range(IMGS):
            sp.dma_start(view[:, 1:1 + H, n, 1:1 + W],
                         self.x[bass.ds(chunk * IMGS + n, 1)].rearrange("o c h w -> (o c) h w")).then_inc(done, 16)


class ChunkLoad:
    dmas = 1

    def __init__(self, kept):
        self.kept = kept

    def __call__(self, sp, xin, chunk, done):
        sp.dma_start(xin[:, IMGS:IMGS + ROWS, 1:1 + W],
                     self.kept[bass.ds(chunk, 1)].rearrange("o c (r w) -> (o c) r w", w=W)).then_inc(done, 16)


class ChunkStore:
    dmas = 1

    def __init__(self, kept):
        self.kept = kept

    def __call__(self, sp, box, chunk, done):
        sp.dma_start(self.kept[bass.ds(chunk, 1)].rearrange("o c x -> (o c) x"), box[:, :]).then_inc(done, 16)


class ImageStores:
    dmas = IMGS

    def __init__(self, kept):
        self.kept = kept

    def __call__(self, sp, box, chunk, done):
        view = box[:, :].rearrange("p (h n w) -> p h n w", n=IMGS, w=W)
        for n in range(IMGS):
            sp.dma_start(self.kept[bass.ds(chunk * IMGS + n, 1)].rearrange("o c (h w) -> (o c) h w", w=W),
                         view[:, :, n, :]).then_inc(done, 16)


def build(nc, x, w_shift1, w_add1, gamma1, beta1, w_shift2, w_add2, gamma2, beta2, wqkv, b_qkv, b_v, router_w,
          router_b, expert_w, expert_b, out):
    images = x.shape[0]
    chunks = images // IMGS
    kept1 = nc.dram_tensor("kept1", (chunks, C, PIX), F32).ap()
    kept2 = nc.dram_tensor("kept2", (images, C, TOK), F32).ap()

    def image_of(t):
        return lambda n: t[bass.ds(n, 1)].rearrange("o c x -> (o c) x")

    with (
        nc.sbuf_tensor("stats1", [C, chunks * BANKS, 6], F32) as stats1,
        nc.sbuf_tensor("stats2", [C, chunks * BANKS, 6], F32) as stats2,
        nc.sbuf_tensor("bn1", [C, 2], F32) as bn1,
        nc.sbuf_tensor("bn2", [C, 2], F32) as bn2,
    ):
        adder_layer(nc, "l1", chunks, ImageLoads(x), None, w_shift1, w_add1, ChunkStore(kept1), stats1)
        batch_norm_scale(nc, "bn1", stats1, gamma1, beta1, bn1[:, 0:1], bn1[:, 1:2])
        adder_layer(nc, "l2", chunks, ChunkLoad(kept1), (bn1[:, 0:1], bn1[:, 1:2]), w_shift2, w_add2,
                    ImageStores(kept2), stats2)
        batch_norm_scale(nc, "bn2", stats2, gamma2, beta2, bn2[:, 0:1], bn2[:, 1:2])

        token_layer(nc, images, image_of(kept2), image_of(x.rearrange("n c h w -> n c (h w)")), bn2[:, 0:1],
                    bn2[:, 1:2], wqkv, b_qkv, b_v.broadcast_to((TT, C)), router_w, router_b.broadcast_to((TT, E)),
                    expert_w, expert_b, image_of(out.rearrange("n c h w -> n c (h w)")))


def kernel(x, L0_conv_w_shift1, L0_conv_w_add1, L0_conv_bn1_gamma, L0_conv_bn1_beta, L0_conv_w_shift2,
           L0_conv_w_add2, L0_conv_bn2_gamma, L0_conv_bn2_beta, L1_attn_W, L1_attn_b, L1_ffn_router_w,
           L1_ffn_router_b, L1_ffn_expert_w, L1_ffn_expert_b):
    import concourse.bacc as bacc
    from concourse.bass_utils import run_bass_kernel_spmd

    def shift_weights(w):
        return np.asarray(w).transpose(1, 2, 3, 0).reshape(C, TAPS * C)

    def add_weights(w):
        return np.asarray(w).transpose(1, 0, 2, 3).reshape(C, C * TAPS)

    def column(v):
        return np.asarray(v).reshape(C, 1)

    arrays = {
        "x": x,
        "w_shift1": shift_weights(L0_conv_w_shift1), "w_add1": add_weights(L0_conv_w_add1),
        "gamma1": column(L0_conv_bn1_gamma), "beta1": column(L0_conv_bn1_beta),
        "w_shift2": shift_weights(L0_conv_w_shift2), "w_add2": add_weights(L0_conv_w_add2),
        "gamma2": column(L0_conv_bn2_gamma), "beta2": column(L0_conv_bn2_beta),
        "wqkv": np.asarray(L1_attn_W).T, "b_qkv": np.asarray(L1_attn_b).reshape(3, C).T,
        "b_v": np.asarray(L1_attn_b).reshape(3, C)[2:3],
        "router_w": L1_ffn_router_w, "router_b": np.asarray(L1_ffn_router_b).reshape(1, E),
        "expert_w": np.asarray(L1_ffn_expert_w).transpose(1, 0, 2).reshape(C, E * C), "expert_b": L1_ffn_expert_b,
    }
    arrays = {k: np.ascontiguousarray(v) for k, v in arrays.items()}
    nc = bacc.Bacc("TRN2", target_bir_lowering=False, num_devices=1)
    aps = [nc.dram_tensor(k, v.shape, F32, kind="ExternalInput").ap() for k, v in arrays.items()]
    out = nc.dram_tensor("out", arrays["x"].shape, F32, kind="ExternalOutput").ap()
    build(nc, *aps, out)
    return run_bass_kernel_spmd(nc, [arrays], core_ids=[0]).results[0]["out"]
```
